# Optimizing a Trainium2 kernel written in Bass

```python
import numpy as np
import jax
import jax.numpy as jnp

def _softmax(x, axis=-1):
    return jax.nn.softmax(x, axis=axis)

def _gelu(x):
    return jax.nn.gelu(x, approximate=True)

def _silu(x):
    return jax.nn.silu(x)

def _sigmoid(x):
    return jax.nn.sigmoid(x)

def _layernorm(x, axis=-1, eps=1e-05):
    m = jnp.mean(x, axis=axis, keepdims=True)
    v = jnp.var(x, axis=axis, keepdims=True)
    return (x - m) / jnp.sqrt(v + eps)

def _scatter_add(tgt, idx, src, axis=0):
    return tgt.at[idx].add(src)

def _segment_sum(src, seg, n):
    return jax.ops.segment_sum(src, seg, n)
kernel_name = 'mk_recurrent_d1_jaxref_r8_c999f0'

def setup_inputs(seed: int=0):
    np.random.seed(seed)
    _w = jnp.asarray

    def _L0_attn_setup():
        import jax, jax.numpy as jnp
        import numpy as np
        H = 512
        D = H // 4
        key = jax.random.key(seed)
        k1, k2, k3, k4, k5 = jax.random.split(key, 5)
        x = jax.random.normal(k1, (4, 512, H), dtype=jnp.float32)
        s_in = 1.0 / np.sqrt(H)
        Wqkv = jax.random.normal(k2, (H, 3 * D), dtype=jnp.float32) * s_in
        bqkv = jax.random.normal(k3, (3 * D,), dtype=jnp.float32) * 0.01
        Wo = jax.random.normal(k4, (D, H), dtype=jnp.float32) * (1.0 / np.sqrt(D))
        bo = jax.random.normal(k5, (H,), dtype=jnp.float32) * 0.01
        return {'x': x, 'Wqkv': Wqkv, 'bqkv': bqkv, 'Wo': Wo, 'bo': bo}
    _L0_attn_in = _L0_attn_setup()

    def _L0_ffn_setup():
        import jax, jax.numpy as jnp
        import numpy as np
        H, FF = (512, 1792)
        B, S = (4, 256)
        key = jax.random.key(seed)
        ks = jax.random.split(key, 7)
        x = jax.random.normal(ks[0], (B, S, H), dtype=jnp.float32)
        gate_t = jax.random.randint(ks[1], (FF, H), -1, 2, dtype=jnp.int32)
        up_t = jax.random.randint(ks[2], (FF, H), -1, 2, dtype=jnp.int32)
        down_t = jax.random.randint(ks[3], (H, FF), -1, 2, dtype=jnp.int32)
        gate_s = jax.random.uniform(ks[4], (FF,), jnp.float32, 0.01, 0.1)
        up_s = jax.random.uniform(ks[5], (FF,), jnp.float32, 0.01, 0.1)
        down_s = jax.random.uniform(ks[6], (H,), jnp.float32, 0.01, 0.1)
        return {'x': x, 'gate_t': gate_t, 'up_t': up_t, 'down_t': down_t, 'gate_s': gate_s, 'up_s': up_s, 'down_s': down_s}
    _L0_ffn_in = _L0_ffn_setup()
    _d = {'L0_attn_x': _L0_attn_in['x'], 'L0_attn_Wqkv': _L0_attn_in['Wqkv'], 'L0_attn_bqkv': _L0_attn_in['bqkv'], 'L0_attn_Wo': _L0_attn_in['Wo'], 'L0_attn_bo': _L0_attn_in['bo'], 'L0_ffn_gate_t': _L0_ffn_in['gate_t'], 'L0_ffn_up_t': _L0_ffn_in['up_t'], 'L0_ffn_down_t': _L0_ffn_in['down_t'], 'L0_ffn_gate_s': _L0_ffn_in['gate_s'], 'L0_ffn_up_s': _L0_ffn_in['up_s'], 'L0_ffn_down_s': _L0_ffn_in['down_s']}
    _x0 = _d['L0_attn_x']
    _d['L0_attn_x'] = jax.random.normal(jax.random.fold_in(jax.random.key(seed), 1), (4, 512, 512), dtype=_x0.dtype)
    del _x0
    return _d

def reference(L0_attn_x, L0_attn_Wqkv, L0_attn_bqkv, L0_attn_Wo, L0_attn_bo, L0_ffn_gate_t, L0_ffn_up_t, L0_ffn_down_t, L0_ffn_gate_s, L0_ffn_up_s, L0_ffn_down_s):

    def _L0_attn_ref(x, Wqkv, bqkv, Wo, bo):
        import jax, jax.numpy as jnp
        import numpy as np
        H = 512
        D = H // 4
        B, S, C = x.shape
        d = C // 4
        qkv = jnp.einsum('bsc,cf->bsf', x, Wqkv) + bqkv
        qkv = qkv.reshape(B, S, 3, d)
        q, k, v = (qkv[:, :, 0], qkv[:, :, 1], qkv[:, :, 2])
        scale = 1.0 / jnp.sqrt(jnp.float32(d)).astype(x.dtype)
        attn = jnp.einsum('bqd,bkd->bqk', q, k) * scale
        attn = jax.nn.softmax(attn, axis=-1)
        out = jnp.einsum('bqk,bkd->bqd', attn, v)
        return jnp.einsum('bqd,dc->bqc', out, Wo) + bo

    def _L0_ffn_ref(x, gate_t, up_t, down_t, gate_s, up_s, down_s):
        import jax, jax.numpy as jnp
        import numpy as np
        H, FF = (512, 1792)
        B, S = (4, 256)
        Bb, Ss, Hh = x.shape
        x_flat = x.reshape(Bb * Ss, Hh)
        gate_w = gate_t.astype(jnp.float32) * gate_s[:, None]
        up_w = up_t.astype(jnp.float32) * up_s[:, None]
        down_w = down_t.astype(jnp.float32) * down_s[:, None]
        gate_out = x_flat @ gate_w.T
        up_out = x_flat @ up_w.T
        hidden = jax.nn.silu(gate_out) * up_out
        out_flat = hidden @ down_w.T
        return out_flat.reshape(Bb, Ss, -1)
    x = L0_attn_x
    xn = _layernorm(x, axis=-1)
    s = _L0_attn_ref(xn, L0_attn_Wqkv, L0_attn_bqkv, L0_attn_Wo, L0_attn_bo)
    g = _silu(_L0_ffn_ref(xn, L0_ffn_gate_t, L0_ffn_up_t, L0_ffn_down_t, L0_ffn_gate_s, L0_ffn_up_s, L0_ffn_down_s))
    x = x + s * g
    return x

_drawn_inputs = setup_inputs


def setup_inputs(seed=0):
    import zlib

    import numpy as np

    out = dict(_drawn_inputs(seed))
    spreads = {}
    factors = {'L0_attn_bqkv': 4.663, 'L0_attn_bo': 5.328}
    for name, (base, spread) in spreads.items():
        noise = np.random.default_rng([zlib.crc32(name.encode()), seed]).standard_normal(out[name].shape)
        drawn = base * np.exp(spread * noise) if base else spread * noise
        out[name] = jnp.asarray(drawn.astype(out[name].dtype))
    for name, factor in factors.items():
        out[name] = (out[name] * factor).astype(out[name].dtype)
    return out
```

```python
from contextlib import ExitStack

import concourse.bass as bass
from concourse import mybir

ALU = mybir.AluOpType
ACT = mybir.ActivationFunctionType
AX_X = mybir.AxisListType.X
F32 = mybir.dt.float32
F16 = mybir.dt.float16
BF16 = mybir.dt.bfloat16
I32 = mybir.dt.int32

P = 128
EPS = 1e-5
XN_SCALE = 1024.0
EXPONENT_BITS = 0x7F800000
RSQRT_MAGIC = 0x5F3759DF


def gated_attention_ffn(nc, x, wqkv, bqkv, wo, bo, gate_t, up_t, down_t, gate_s, up_s, down_s, out):
    B, S, H = x.shape
    D = wo.shape[0]
    FF = gate_t.shape[1]
    TT = S // P
    HC = H // P
    FC = FF // P
    SM_SCALE = float(D) ** -0.5
    FIRST = 0
    PRIMED = 1
    assert D == P and S == 512 and H == 512 and FF % P == 0 and HC == B and TT == 4

    with ExitStack() as ctx:
        def sb(name, shape, dt):
            return ctx.enter_context(nc.sbuf_tensor(name, shape, dt))

        def sem(name):
            return ctx.enter_context(nc.semaphore(name))

        wqkv_sb = sb("wqkv_sb", [P, HC, 3 * D], F32)
        wo_sb = sb("wo_sb", [P, H], F32)
        bqkv_sb = sb("bqkv_sb", [P, 3], F32)
        bo_row = sb("bo_row", [P, H], F32)
        down_s_row = sb("down_s_row", [P, H], F32)
        half_down_s = sb("half_down_s", [P, H], F32)
        gate_s_sb = sb("gate_s_sb", [P, FC], F32)
        up_s_sb = sb("up_s_sb", [P, FC], F32)
        tanh_scale = sb("tanh_scale", [P, FC], F32)
        gu_scale = sb("gu_scale", [P, FC], F32)
        gu_exponent = sb("gu_exponent", [P, FC], F32)
        hid_shrink = sb("hid_shrink", [P, FC], F32)
        hid_grow = sb("hid_grow", [P, FC], F32)
        gu_hid = sb("gu_hid", [P, FC], F32)
        hid_scale = sb("hid_scale", [P, FC], F32)
        identity = sb("identity", [P, P], F32)
        hid_sb = sb("hid_sb", [P, 2, FC, S], F16)
        hid_hi, hid_lo = hid_sb[:, 0], hid_sb[:, 1]
        w_stage = hid_sb[:].rearrange("p a c s -> p (a c s)").bitcast(I32)[:, 0:3 * FF].rearrange(
            "p (n f) -> p n f", n=3)
        gate_w = sb("gate_w", [P, HC, FF], F16)
        up_w = sb("up_w", [P, HC, FF], F16)
        down_w = sb("down_w", [P, FC, H], BF16)
        xn_hi = sb("xn_hi", [P, B, HC, S], F16)
        xn_lo = sb("xn_lo", [P, B, HC, S], F16)
        attn = sb("attn", [P, B, TT, H], F32)
        x_sb = sb("x_sb", [P, TT, H], F32)
        xn = sb("xn", [P, TT, H], F32)
        xnT = sb("xnT", [P, HC, S], F32)
        stats = sb("stats", [P, TT, 6], F32)
        mean_sum = sb("mean_sum", [P, TT], F32)
        mean_gap = sb("mean_gap", [P, TT], F32)
        square_sum = sb("square_sum", [P, TT], F32)
        gap_square = sb("gap_square", [P, TT], F32)
        mean = sb("mean", [P, TT], F32)
        var = sb("var", [P, TT], F32)
        var_eps = sb("var_eps", [P, TT], F32)
        rs_bits = sb("rs_bits", [P, TT], I32)
        rs_y = sb("rs_y", [P, 4, TT], F32)
        rs_t = sb("rs_t", [P, 3, TT], F32)
        rs_u = sb("rs_u", [P, 3, TT], F32)
        rstd = sb("rstd", [P, TT], F32)
        qT = sb("qT", [P, S], F32)
        kT = sb("kT", [P, S], F32)
        v = sb("v", [P, TT, D], F32)
        row_max = sb("row_max", [P, TT], F32)
        neg_max = sb("neg_max", [P, TT], F32)
        row_sum = sb("row_sum", [P, TT], F32)
        inv_sum = sb("inv_sum", [P, TT], F32)
        e_sb = sb("e_sb", [P, TT, S], F32)
        probs = sb("probs", [P, TT, S], F32)
        probsT = sb("probsT", [P, TT, S], F32)
        oT = sb("oT", [P, S], F32)
        gate_tanh = e_sb[:, 0:2, :]
        gate_act = e_sb[:, 2:4, :]
        hidden = probs[:, 0:2, :]
        half_y = probs[:, 2:4, :]
        y_tanh = probsT[:, 0:2, :]
        y_silu = probsT[:, 2:4, :]
        mixed = xn[:, 0:2, :]
        out_sb = xnT

        psum = ctx.enter_context(nc.psum_tensor("psum", [P, 8, 512], F32))
        turn_bank = lambda j: psum[:, j % 2, :]
        QV_BANK, KO_BANK = psum[:, 2, :], psum[:, 3, :]
        row_bank = lambda t: psum[:, 4 + t, :]
        gate_bank = lambda c: psum[:, c % 2, :]
        up_bank = lambda c: psum[:, 2 + c % 2, :]
        down_bank = lambda t: psum[:, 4 + t % 2, :]

        x_loaded = [sem(f"x_loaded{t}") for t in range(TT)]
        w_loaded = [sem(f"w_loaded{n}") for n in range(3)]
        wqkv_loaded = sem("wqkv_loaded")
        wo_loaded = sem("wo_loaded")
        bqkv_loaded = sem("bqkv_loaded")
        rows_loaded = sem("rows_loaded")
        scales_loaded = sem("scales_loaded")
        out_stored = [sem(f"out_stored{t}") for t in range(TT)]
        identity_made = sem("identity_made")
        scales_made = sem("scales_made")
        rows_made = sem("rows_made")
        w_cast = sem("w_cast")
        ln_step = sem("ln_step")
        xn_made = sem("xn_made")
        xt_full = sem("xt_full")
        xt_read = sem("xt_read")
        xhi_made = sem("xhi_made")
        xlo_made = sem("xlo_made")
        q_full = sem("q_full")
        k_full = sem("k_full")
        v_full = sem("v_full")
        q_read = sem("q_read")
        k_read = sem("k_read")
        v_read = sem("v_read")
        scores_full = sem("scores_full")
        max_made = sem("max_made")
        negmax_made = sem("negmax_made")
        exp_made = sem("exp_made")
        inv_made = sem("inv_made")
        probs_made = sem("probs_made")
        pt_full = sem("pt_full")
        pt_read = sem("pt_read")
        o_full = sem("o_full")
        o_read = sem("o_read")
        wo_full = sem("wo_full")
        attn_made = sem("attn_made")
        gu_full = sem("gu_full")
        gtanh_made = sem("gtanh_made")
        gact_made = sem("gact_made")
        hidden_made = sem("hidden_made")
        hi_made = sem("hi_made")
        lo_made = sem("lo_made")
        down_full = sem("down_full")
        halfy_made = sem("halfy_made")
        ytanh_made = sem("ytanh_made")
        ysilu_made = sem("ysilu_made")
        mixed_made = sem("mixed_made")
        out_made = sem("out_made")

        x_tiles = x.rearrange("b (t p) h -> b t p h", p=P)
        out_tiles = out.rearrange("b (t p) h -> b t p h", p=P)
        gate_rows = gate_t.rearrange("(c p) f -> c p f", p=P)
        up_rows = up_t.rearrange("(c p) f -> c p f", p=P)

        block = ctx.enter_context(nc.Block())

        @block.sync
        def _(sp):
            def load_x(b, t):
                sp.dma_start(x_sb[:, t, :], x_tiles[b, t]).then_inc(x_loaded[t], 16)

            def load_w(b):
                for n, src in enumerate((gate_rows[b], up_rows[b], down_t[b])):
                    sp.dma_start(w_stage[:, n, :], src).then_inc(w_loaded[n], 16)

            for t in range(TT):
                load_x(0, t)
            sp.dma_start(wqkv_sb[:], wqkv.rearrange("(c p) f -> p c f", p=P)).then_inc(wqkv_loaded, 16)
            sp.dma_start(bqkv_sb[:], bqkv).then_inc(bqkv_loaded, 16)
            for t in range(TT):
                sp.wait_ge(xn_made, t + 1)
                load_x(1, t)
            sp.dma_start(gate_s_sb[:], gate_s).then_inc(scales_loaded, 16)
            sp.dma_start(up_s_sb[:], up_s).then_inc(scales_loaded, 16)
            load_w(0)
            sp.dma_start(wo_sb[:], wo).then_inc(wo_loaded, 16)
            sp.dma_start(bo_row[:], bo.to_broadcast([P, H])).then_inc(rows_loaded, 16)
            sp.dma_start(down_s_row[:], down_s.to_broadcast([P, H])).then_inc(rows_loaded, 16)
            with sp.Fori(1, B - 1) as b:
                for t in range(TT):
                    sp.wait_ge(xn_made, b * TT + (t + 1))
                    load_x(b + 1, t)
                sp.wait_ge(w_cast, 3 * b)
                load_w(b)
            sp.wait_ge(w_cast, 3 * (B - 1))
            load_w(B - 1)

            sp.wait_ge(xn_made, B * TT)
            for t in range(TT):
                load_x(0, t)

            def store_group(i):
                for t in range(TT):
                    sp.wait_ge(out_made, i * TT + (t + 1))
                    sp.dma_start(out_tiles[i, t], out_sb[:, t, :]).then_inc(out_stored[t], 16)

            with sp.Fori(0, B - 1) as i:
                store_group(i)
                for t in range(TT):
                    sp.wait_ge(out_stored[t], (i + 1) * 16)
                    load_x(i + 1, t)
            store_group(B - 1)
            for t in range(TT):
                sp.wait_ge(out_stored[t], B * 16)

        @block.gpsimd
        def _(pool):
            nc.gpsimd.memset(identity[:], 0.0).then_inc(identity_made, 1)
            pool.wait_ge(identity_made, 1)
            nc.gpsimd.affine_select(out=identity[:], in_=identity[:], compare_op=ALU.not_equal, fill=1.0,
                                    base=0, pattern=[[-1, P]], channel_multiplier=1).then_inc(identity_made, 1)
            with pool.Fori(0, B) as b:
                for j in range(HC):
                    pool.wait_ge(xhi_made, b * HC + (j + 1))
                    nc.gpsimd.tensor_tensor(xn_lo[:, b, j, :], xnT[:, j, :], xn_hi[:, b, j, :],
                                            ALU.subtract).then_inc(xlo_made, 1)
            with pool.Fori(0, B) as i:
                for c in range(FC):
                    pool.wait_ge(hi_made, i * FC + (c + 1))
                    nc.gpsimd.tensor_tensor(hid_lo[:, c, :], hidden[:, c % 2, :], hid_hi[:, c, :],
                                            ALU.subtract).then_inc(lo_made, 1)
                for t in range(TT):
                    pool.wait_ge(ysilu_made, i * TT + (t + 1))
                    nc.gpsimd.tensor_tensor(mixed[:, t % 2, :], y_silu[:, t % 2, :], attn[:, i, t, :],
                                            ALU.mult).then_inc(mixed_made, 1)
                    pool.wait_ge(mixed_made, i * TT + (t + 1))
                    pool.wait_ge(x_loaded[t], (i + (B + 1)) * 16)
                    nc.gpsimd.tensor_tensor(out_sb[:, t, :], mixed[:, t % 2, :], x_sb[:, t, :],
                                            ALU.add).then_inc(out_made, 1)

        @block.scalar
        def _(act):
            def evacuate_xt(b):
                for j in range(HC):
                    act.wait_ge(xt_full, b * HC + (j + 1))
                    if j == 0 and b is not FIRST:
                        act.wait_ge(xlo_made, b * HC)
                    nc.scalar.activation(xnT[:, j, :], turn_bank(j), ACT.Copy).then_inc(xt_read, 1)

            def evacuate_q(b):
                act.wait_ge(q_full, b + 1)
                nc.scalar.activation(qT[:], QV_BANK, ACT.Identity, bias=bqkv_sb[:, 0:1],
                                     scale=1.0 / XN_SCALE).then_inc(q_read, 1)

            def evacuate_k(b):
                act.wait_ge(k_full, b + 1)
                nc.scalar.activation(kT[:], KO_BANK, ACT.Identity, bias=bqkv_sb[:, 1:2],
                                     scale=1.0 / XN_SCALE).then_inc(k_read, 1)

            def evacuate_v(b):
                act.wait_ge(v_full, b + 1)
                nc.scalar.activation(v[:].rearrange("p t d -> p (t d)"), QV_BANK, ACT.Copy,
                                     scale=1.0 / XN_SCALE).then_inc(v_read, 1)

            def attend(b, with_next):
                if with_next:
                    evacuate_xt(b + 1)
                for t in range(TT):
                    act.wait_ge(negmax_made, b * TT + (t + 1))
                    nc.scalar.activation(e_sb[:, t, :], row_bank(t), ACT.Exp, bias=neg_max[:, t:t + 1],
                                         scale=SM_SCALE, accum_out=row_sum[:, t:t + 1]).then_inc(exp_made, 1)
                if with_next:
                    evacuate_q(b + 1)
                    evacuate_k(b + 1)
                for j in range(TT):
                    act.wait_ge(pt_full, b * TT + (j + 1))
                    nc.scalar.activation(probsT[:, j, :], turn_bank(j), ACT.Copy).then_inc(pt_read, 1)
                act.wait_ge(o_full, b + 1)
                nc.scalar.activation(oT[:], KO_BANK, ACT.Identity, bias=bqkv_sb[:, 2:3]).then_inc(o_read, 1)
                if with_next:
                    evacuate_v(b + 1)

            evacuate_xt(FIRST)
            act.wait_ge(bqkv_loaded, 16)
            evacuate_q(0)
            evacuate_k(0)
            evacuate_v(0)
            with act.Fori(0, B - 1) as b:
                attend(b, True)
            attend(B - 1, False)

            with act.Fori(0, B) as i:
                for c in range(FC):
                    act.wait_ge(gu_full, i * FC + (c + 1))
                    nc.scalar.activation(gate_tanh[:, c % 2, :], gate_bank(c), ACT.Tanh,
                                         scale=tanh_scale[:, c:c + 1]).then_inc(gtanh_made, 1)
                    act.wait_ge(hidden_made, i * FC + (c + 1))
                    nc.scalar.activation(hid_hi[:, c, :], hidden[:, c % 2, :], ACT.Copy).then_inc(hi_made, 1)
                for t in range(TT):
                    act.wait_ge(halfy_made, i * TT + (t + 1))
                    nc.scalar.activation(y_tanh[:, t % 2, :], half_y[:, t % 2, :],
                                         ACT.Tanh).then_inc(ytanh_made, 1)

        @block.vector
        def _(dve):
            LN_SELF = 4 + 3 + 3 * 3 + 1

            def layernorm(b):
                for t in range(TT):
                    dve.wait_ge(x_loaded[t], (b + 1) * 16)
                    last = nc.vector.bn_stats(stats[:, t, :], x_sb[:, t, :])
                last.then_inc(ln_step, 1)
                n = 1
                dve.wait_ge(ln_step, b * LN_SELF + n)
                mean_e, mean_o = stats[:, :, 1], stats[:, :, 4]
                nc.vector.tensor_tensor(mean_sum[:], mean_e, mean_o, ALU.add)
                nc.vector.tensor_tensor(mean_gap[:], mean_e, mean_o, ALU.subtract)
                nc.vector.tensor_tensor(square_sum[:], stats[:, :, 2], stats[:, :, 5], ALU.add).then_inc(ln_step, 1)
                n += 1
                dve.wait_ge(ln_step, b * LN_SELF + n)
                nc.vector.tensor_scalar(mean[:], mean_sum[:], 0.5, None, ALU.mult)
                nc.vector.scalar_tensor_tensor(out=gap_square[:], in0=mean_gap[:], scalar=0.25, in1=mean_gap[:],
                                               op0=ALU.mult, op1=ALU.mult).then_inc(ln_step, 1)
                n += 1
                dve.wait_ge(ln_step, b * LN_SELF + n)
                nc.vector.scalar_tensor_tensor(out=var[:], in0=square_sum[:], scalar=1.0 / H, in1=gap_square[:],
                                               op0=ALU.mult, op1=ALU.add).then_inc(ln_step, 1)
                n += 1
                dve.wait_ge(ln_step, b * LN_SELF + n)
                nc.vector.tensor_scalar(var_eps[:], var[:], EPS, None, ALU.add).then_inc(ln_step, 1)
                n += 1
                dve.wait_ge(ln_step, b * LN_SELF + n)
                nc.vector.tensor_scalar(rs_bits[:], var_eps[:].bitcast(I32), 1, None,
                                        ALU.logical_shift_right).then_inc(ln_step, 1)
                n += 1
                dve.wait_ge(ln_step, b * LN_SELF + n)
                nc.vector.tensor_scalar(rs_y[:, 0, :].bitcast(I32), rs_bits[:], -1.0, float(RSQRT_MAGIC),
                                        ALU.mult, ALU.add).then_inc(ln_step, 1)
                n += 1
                for k in range(3):
                    dve.wait_ge(ln_step, b * LN_SELF + n)
                    nc.vector.tensor_tensor(rs_t[:, k, :], rs_y[:, k, :], rs_y[:, k, :],
                                            ALU.mult).then_inc(ln_step, 1)
                    n += 1
                    dve.wait_ge(ln_step, b * LN_SELF + n)
                    nc.vector.scalar_tensor_tensor(out=rs_u[:, k, :], in0=rs_t[:, k, :], scalar=-0.5,
                                                   in1=var_eps[:], op0=ALU.mult, op1=ALU.mult).then_inc(ln_step, 1)
                    n += 1
                    dve.wait_ge(ln_step, b * LN_SELF + n)
                    nc.vector.scalar_tensor_tensor(out=rs_y[:, k + 1, :], in0=rs_u[:, k, :], scalar=1.5,
                                                   in1=rs_y[:, k, :], op0=ALU.add, op1=ALU.mult).then_inc(ln_step, 1)
                    n += 1
                dve.wait_ge(ln_step, b * LN_SELF + n)
                nc.vector.tensor_scalar(rstd[:], rs_y[:, 3, :], XN_SCALE, None, ALU.mult).then_inc(ln_step, 1)
                n += 1
                assert n == LN_SELF
                dve.wait_ge(ln_step, b * LN_SELF + n)
                if b is not FIRST:
                    dve.wait_ge(xt_full, b * HC)
                for t in range(TT):
                    nc.vector.tensor_scalar(xn[:, t, :], x_sb[:, t, :], mean[:, t:t + 1], rstd[:, t:t + 1],
                                            ALU.subtract, ALU.mult).then_inc(xn_made, 1)

            def take_hi(b):
                for j in range(HC):
                    dve.wait_ge(xt_read, b * HC + (j + 1))
                    nc.vector.tensor_copy(xn_hi[:, b, j, :], xnT[:, j, :]).then_inc(xhi_made, 1)

            def normalize(b, t):
                dve.wait_ge(exp_made, b * TT + (t + 1))
                nc.vector.reciprocal(inv_sum[:, t:t + 1], row_sum[:, t:t + 1]).then_inc(inv_made, 1)
                dve.wait_ge(inv_made, b * TT + (t + 1))
                nc.vector.tensor_scalar(probs[:, t, :], e_sb[:, t, :], inv_sum[:, t:t + 1], None,
                                        ALU.mult).then_inc(probs_made, 1)

            def softmax(b):
                for t in range(TT):
                    dve.wait_ge(scores_full, b * TT + (t + 1))
                    nc.vector.reduce_max(row_max[:, t:t + 1], row_bank(t), AX_X).then_inc(max_made, 1)
                    dve.wait_ge(max_made, b * TT + (t + 1))
                    nc.vector.tensor_scalar(neg_max[:, t:t + 1], row_max[:, t:t + 1], -SM_SCALE, None,
                                            ALU.mult).then_inc(negmax_made, 1)
                    if t >= 1:
                        normalize(b, t - 1)
                normalize(b, TT - 1)

            def turn_weights(b):
                for n, dst in enumerate((gate_w[:, b, :], up_w[:, b, :])):
                    dve.wait_ge(w_loaded[n], (b + 1) * 16)
                    nc.vector.tensor_copy(dst, w_stage[:, n, :]).then_inc(w_cast, 1)
                dve.wait_ge(w_loaded[2], (b + 1) * 16)
                nc.vector.tensor_tensor(down_w[:, :, bass.ts(b, H // B)],
                                        w_stage[:, 2, :].rearrange("p (c h) -> p c h", c=FC),
                                        hid_grow[:].unsqueeze(2).to_broadcast([P, FC, H // B]),
                                        ALU.mult).then_inc(w_cast, 1)

            def attend(b, with_next, with_layernorm):
                if with_next:
                    take_hi(b + 1)
                softmax(b)
                if with_layernorm:
                    layernorm(b + 2)
                turn_weights(b)
                for t in range(TT):
                    dve.wait_ge(wo_full, b * TT + (t + 1))
                    nc.vector.tensor_tensor(attn[:, b, t, :], row_bank(t), bo_row[:],
                                            ALU.add).then_inc(attn_made, 1)

            dve.sem_inc(attn_made, PRIMED)
            layernorm(FIRST)
            take_hi(0)
            layernorm(1)

            dve.wait_ge(scales_loaded, 32)
            nc.vector.tensor_scalar(tanh_scale[:], gate_s_sb[:], 0.5 / XN_SCALE, None,
                                    ALU.mult).then_inc(scales_made, 1)
            nc.vector.tensor_tensor(gu_scale[:], gate_s_sb[:], up_s_sb[:], ALU.mult).then_inc(scales_made, 1)
            dve.wait_ge(scales_made, 2)
            nc.vector.tensor_scalar(gu_exponent[:].bitcast(I32), gu_scale[:].bitcast(I32), EXPONENT_BITS, None,
                                    ALU.bitwise_and).then_inc(scales_made, 1)
            dve.wait_ge(scales_made, 3)
            nc.vector.tensor_scalar(hid_shrink[:].bitcast(I32), gu_exponent[:].bitcast(I32), -1.0,
                                    float(0x7F000000), ALU.mult, ALU.add).then_inc(scales_made, 1)
            nc.vector.tensor_scalar(hid_grow[:], gu_exponent[:], 16.0, None, ALU.mult).then_inc(scales_made, 1)
            dve.wait_ge(scales_made, 5)
            nc.vector.tensor_tensor(gu_hid[:], gu_scale[:], hid_shrink[:], ALU.mult).then_inc(scales_made, 1)
            dve.wait_ge(scales_made, 6)
            nc.vector.tensor_scalar(hid_scale[:], gu_hid[:], 0.5 / 16.0 / XN_SCALE / XN_SCALE, None,
                                    ALU.mult).then_inc(scales_made, 1)
            dve.wait_ge(rows_loaded, 32)
            nc.vector.tensor_scalar(half_down_s[:], down_s_row[:], 0.5, None, ALU.mult).then_inc(rows_made, 1)

            with dve.Fori(0, B - 2) as b:
                attend(b, True, True)
            attend(B - 2, True, False)
            attend(B - 1, False, False)

            dve.wait_ge(scales_made, 7)
            dve.wait_ge(rows_made, 1)
            with dve.Fori(0, B) as i:
                for c in range(FC):
                    dve.wait_ge(gtanh_made, i * FC + (c + 1))
                    nc.vector.scalar_tensor_tensor(out=gate_act[:, c % 2, :], in0=gate_tanh[:, c % 2, :], scalar=1.0,
                                                   in1=gate_bank(c), op0=ALU.add, op1=ALU.mult).then_inc(gact_made, 1)
                    dve.wait_ge(gact_made, i * FC + (c + 1))
                    if c >= 2:
                        dve.wait_ge(lo_made, i * FC + (c - 1))
                    nc.vector.scalar_tensor_tensor(out=hidden[:, c % 2, :], in0=gate_act[:, c % 2, :],
                                                   scalar=hid_scale[:, c:c + 1], in1=up_bank(c),
                                                   op0=ALU.mult, op1=ALU.mult).then_inc(hidden_made, 1)
                for t in range(TT):
                    dve.wait_ge(down_full, i * TT + (t + 1))
                    if t >= 2:
                        dve.wait_ge(ysilu_made, i * TT + (t - 1))
                    nc.vector.tensor_tensor(half_y[:, t % 2, :], down_bank(t), half_down_s[:],
                                            ALU.mult).then_inc(halfy_made, 1)
                    dve.wait_ge(ytanh_made, i * TT + (t + 1))
                    if t >= 2:
                        dve.wait_ge(mixed_made, i * TT + (t - 1))
                    nc.vector.scalar_tensor_tensor(out=y_silu[:, t % 2, :], in0=y_tanh[:, t % 2, :], scalar=1.0,
                                                   in1=half_y[:, t % 2, :], op0=ALU.add,
                                                   op1=ALU.mult).then_inc(ysilu_made, 1)

        @block.tensor
        def _(pe):
            def transpose_xn(b):
                for j in range(HC):
                    if j >= 2:
                        pe.wait_ge(xt_read, b * HC + (j - 1))
                    for t in range(TT):
                        if j == 0:
                            pe.wait_ge(xn_made, b * TT + (t + 1))
                        last = nc.tensor.transpose(turn_bank(j)[:, bass.ts(t, P)], xn[:, t, bass.ts(j, P)],
                                                   identity[:])
                    last.then_inc(xt_full, 1)

            def project_q(b):
                pe.wait_ge(xt_read, (b + 1) * HC)
                if b is not FIRST:
                    pe.wait_ge(v_read, b)
                for j in range(HC):
                    last = nc.tensor.matmul(QV_BANK, wqkv_sb[:, j, 0:D], xnT[:, j, :],
                                            start=(j == 0), stop=(j == HC - 1))
                last.then_inc(q_full, 1)

            def project_k(b):
                for j in range(HC):
                    last = nc.tensor.matmul(KO_BANK, wqkv_sb[:, j, D:2 * D], xnT[:, j, :],
                                            start=(j == 0), stop=(j == HC - 1))
                last.then_inc(k_full, 1)

            def project_v(b, tiles):
                for t in tiles:
                    if t == 0:
                        pe.wait_ge(q_read, b + 1)
                    for j in range(HC):
                        last = nc.tensor.matmul(QV_BANK[:, bass.ts(t, D)], xnT[:, j, bass.ts(t, P)],
                                                wqkv_sb[:, j, 2 * D:3 * D], start=(j == 0), stop=(j == HC - 1))
                    if t == TT - 1:
                        last.then_inc(v_full, 1)

            def transpose_probs(b, chunks):
                for j in chunks:
                    if j >= 2:
                        pe.wait_ge(pt_read, b * TT + (j - 1))
                    for t in range(TT):
                        if j == 0:
                            pe.wait_ge(probs_made, b * TT + (t + 1))
                        last = nc.tensor.transpose(turn_bank(j)[:, bass.ts(t, P)], probs[:, t, bass.ts(j, P)],
                                                   identity[:])
                    last.then_inc(pt_full, 1)

            def attend(b, with_next):
                if with_next:
                    transpose_xn(b + 1)
                pe.wait_ge(k_read, b + 1)
                pe.wait_ge(attn_made, b * TT + PRIMED)
                for t in range(TT):
                    nc.tensor.matmul(row_bank(t), qT[:, bass.ts(t, P)], kT[:], start=True,
                                     stop=True).then_inc(scores_full, 1)
                if with_next:
                    project_q(b + 1)
                    project_k(b + 1)
                    pe.wait_ge(xt_read, (b + 2) * HC)
                transpose_probs(b, range(0, 2))
                if with_next:
                    project_v(b + 1, range(0, TT // 2))
                transpose_probs(b, range(2, TT))
                pe.wait_ge(v_read, b + 1)
                if with_next:
                    pe.wait_ge(k_read, b + 2)
                for j in range(TT):
                    pe.wait_ge(pt_read, b * TT + (j + 1))
                    last = nc.tensor.matmul(KO_BANK, v[:, j, :], probsT[:, j, :], start=(j == 0), stop=(j == TT - 1))
                last.then_inc(o_full, 1)
                if with_next:
                    project_v(b + 1, range(TT // 2, TT))
                pe.wait_ge(o_read, b + 1)
                for t in range(TT):
                    nc.tensor.matmul(row_bank(t), oT[:, bass.ts(t, P)], wo_sb[:], start=True,
                                     stop=True).then_inc(wo_full, 1)

            pe.wait_ge(identity_made, 2)
            transpose_xn(0)
            pe.wait_ge(wqkv_loaded, 16)
            project_q(FIRST)
            project_k(0)
            project_v(0, range(TT))
            pe.wait_ge(wo_loaded, 16)
            with pe.Fori(0, B - 1) as b:
                attend(b, True)
            attend(B - 1, False)

            pe.wait_ge(w_cast, 3 * B)
            pe.wait_ge(xlo_made, HC * B)
            pe.wait_ge(attn_made, TT * B + PRIMED)
            with pe.Fori(0, B) as i:
                for c in range(FC):
                    if c >= 2:
                        pe.wait_ge(hidden_made, i * FC + (c - 1))
                    for bank, w in ((gate_bank(c), gate_w), (up_bank(c), up_w)):
                        for j in range(HC):
                            for half in (xn_hi, xn_lo):
                                last = nc.tensor.matmul(bank, w[:, j, bass.ts(c, P)], half[:, i, j, :],
                                                        start=(j == 0 and half is xn_hi),
                                                        stop=(j == HC - 1 and half is xn_lo))
                    last.then_inc(gu_full, 1)
                for t in range(TT):
                    if t >= 2:
                        pe.wait_ge(halfy_made, i * TT + (t - 1))
                    for c in range(FC):
                        if t == 0:
                            pe.wait_ge(lo_made, i * FC + (c + 1))
                        for half in (hid_hi, hid_lo):
                            last = nc.tensor.matmul(down_bank(t), half[:, c, bass.ts(t, P)], down_w[:, c, :],
                                                    start=(c == 0 and half is hid_hi),
                                                    stop=(c == FC - 1 and half is hid_lo))
                    last.then_inc(down_full, 1)


def kernel(**inputs):
    import numpy as np
    import concourse.bacc as bacc
    from concourse.bass_utils import run_bass_kernel_spmd

    a = {name.removeprefix("L0_"): np.asarray(value) for name, value in inputs.items()}
    B, S, H = a["attn_x"].shape
    FF = a["ffn_gate_t"].shape[0]
    arrays = {
        "x": a["attn_x"],
        "wqkv": a["attn_Wqkv"],
        "bqkv": a["attn_bqkv"].reshape(3, P).T,
        "wo": a["attn_Wo"],
        "bo": a["attn_bo"].reshape(1, H),
        "gate_t": a["ffn_gate_t"].T,
        "up_t": a["ffn_up_t"].T,
        "down_t": a["ffn_down_t"].reshape(B, H // B, FF // P, P).transpose(0, 3, 2, 1).reshape(B, P, FF),
        "gate_s": a["ffn_gate_s"].reshape(FF // P, P).T,
        "up_s": a["ffn_up_s"].reshape(FF // P, P).T,
        "down_s": a["ffn_down_s"].reshape(1, H),
    }
    nc = bacc.Bacc("TRN2", target_bir_lowering=False, num_devices=1)
    named, args = {}, []
    for name, value in arrays.items():
        value = np.ascontiguousarray(value)
        named[f"in_{name}"] = value
        args.append(nc.dram_tensor(f"in_{name}", value.shape, mybir.dt.from_np(value.dtype), kind="ExternalInput").ap())
    args.append(nc.dram_tensor("out_0", (B, S, H), F32, kind="ExternalOutput").ap())
    gated_attention_ffn(nc, *args)
    result = run_bass_kernel_spmd(nc, [named], core_ids=[0])
    return result.results[0]["out_0"]
```

```python
from contextlib import ExitStack

import concourse.bass as bass
from concourse import mybir

ALU = mybir.AluOpType
ACT = mybir.ActivationFunctionType
AX_X = mybir.AxisListType.X
F32 = mybir.dt.float32
F16 = mybir.dt.float16
BF16 = mybir.dt.bfloat16
I32 = mybir.dt.int32

P = 128
EPS = 1e-5
XN_SCALE = 2.0**10
W_SCALE = 2.0**14
QKV_SCALE = 2.0**-4
PROBS_SCALE = 2.0**14
HID_SCALE = 2.0**-17
EXPONENT_BITS = 0x7F800000
RSQRT_MAGIC = 0x5F3759DF


def gated_attention_ffn(nc, x, wqkv, bqkv, wo, bo, gate_t, up_t, down_t, gate_s, up_s, down_s, out):
    B, S, H = x.shape
    D = wo.shape[0]
    FF = gate_t.shape[1]
    TT = S // P
    HC = H // P
    FC = FF // P
    SM_SCALE = float(D) ** -0.5
    NORM_STEPS = 6
    PRIMED = 1
    assert D == P and S == 512 and H == 512 and FF % P == 0 and HC == B and TT == 4

    with ExitStack() as ctx:
        def sb(name, shape, dt):
            return ctx.enter_context(nc.sbuf_tensor(name, shape, dt))

        def sem(name):
            return ctx.enter_context(nc.semaphore(name))

        wqkv_sb = sb("wqkv_sb", [P, HC, 3 * D], F32)
        wo_sb = sb("wo_sb", [P, H], F32)
        wqkv_hi = sb("wqkv_hi", [P, HC, 3 * D], F16)
        wqkv_lo = sb("wqkv_lo", [P, HC, 3 * D], F16)
        wo_hi = sb("wo_hi", [P, H], F16)
        wo_lo = sb("wo_lo", [P, H], F16)
        bqkv_sb = sb("bqkv_sb", [P, 3], F32)
        bias = sb("bias", [P, 3], F32)
        square_parts = sb("square_parts", [P, 4], F32)
        square_sums = sb("square_sums", [P, 4], F32)
        norm_square = sb("norm_square", [P, 3], F32)
        norm_bits = sb("norm_bits", [P, 3], I32)
        norm_guess = sb("norm_guess", [P, 3], I32)
        norm_inverse = sb("norm_inverse", [P, 3], F32)
        w_scale = sb("w_scale", [P, 3], F32)
        w_unscale = sb("w_unscale", [P, 3], F32)
        score_scale = sb("score_scale", [P, 1], F32)
        neg_score_scale = sb("neg_score_scale", [P, 1], F32)
        attn_scale = sb("attn_scale", [P, 1], F32)
        bo_row = sb("bo_row", [P, H], F32)
        half_down_s = sb("half_down_s", [P, H], F32)
        gate_s_sb = sb("gate_s_sb", [P, FC], F32)
        up_s_sb = sb("up_s_sb", [P, FC], F32)
        tanh_scale = sb("tanh_scale", [P, FC], F32)
        gu_scale = sb("gu_scale", [P, FC], F32)
        hid_scale = sb("hid_scale", [P, FC], F32)
        identity = sb("identity", [P, P], F32)
        ones = sb("ones", [P, P], F32)
        hid_sb = sb("hid_sb", [P, 2, FC, S], F16)
        hid_hi, hid_lo = hid_sb[:, 0], hid_sb[:, 1]
        w_stage = hid_sb[:].rearrange("p a c s -> p (a c s)").bitcast(I32)[:, 0:3 * FF].rearrange(
            "p (n f) -> p n f", n=3)
        gate_w = sb("gate_w", [P, HC, FF], F16)
        up_w = sb("up_w", [P, HC, FF], F16)
        down_w = sb("down_w", [P, FC, H], F16)
        xn_hi = sb("xn_hi", [P, B, HC, S], F16)
        xn_lo = sb("xn_lo", [P, B, HC, S], F16)
        attn = sb("attn", [P, B, TT, H], F32)
        x_sb = sb("x_sb", [P, TT, H], F32)
        xn = sb("xn", [P, TT, H], F32)
        xnT = sb("xnT", [P, HC, S], F32)
        stats = sb("stats", [P, TT, 6], F32)
        mean_sum = sb("mean_sum", [P, TT], F32)
        mean_gap = sb("mean_gap", [P, TT], F32)
        square_sum = sb("square_sum", [P, TT], F32)
        gap_square = sb("gap_square", [P, TT], F32)
        mean = sb("mean", [P, TT], F32)
        var = sb("var", [P, TT], F32)
        var_eps = sb("var_eps", [P, TT], F32)
        rs_bits = sb("rs_bits", [P, TT], I32)
        rs_y = sb("rs_y", [P, 4, TT], F32)
        rs_t = sb("rs_t", [P, 3, TT], F32)
        rs_u = sb("rs_u", [P, 3, TT], F32)
        rstd = sb("rstd", [P, TT], F32)
        qkv_f32 = wqkv_sb[:].rearrange("p c f -> p (c f)").rearrange("p (n s) -> p n s", n=3)
        o_f32 = wo_sb
        qkv_hi = sb("qkv_hi", [P, 3, S], F16)
        qkv_lo = sb("qkv_lo", [P, 3, S], F16)
        row_max = sb("row_max", [P, TT], F32)
        neg_max = sb("neg_max", [P, TT], F32)
        row_sum = sb("row_sum", [P, TT], F32)
        inv_sum = sb("inv_sum", [P, TT], F32)
        probs = sb("probs", [P, TT, S], F32)
        pt_sb = sb("pt_sb", [P, 2, TT, S], F16)
        pt_hi, pt_lo = pt_sb[:, 0], pt_sb[:, 1]
        oT_hi = sb("oT_hi", [P, S], F16)
        oT_lo = sb("oT_lo", [P, S], F16)
        gate_tanh = xn[:, 0:2, :]
        gate_act = xn[:, 2:4, :]
        hidden = qkv_f32[:, 0:2, :]
        half_y = probs[:, 0:2, :]
        y_tanh = probs[:, 2:4, :]
        pt_f32 = pt_sb[:].rearrange("p a j s -> p (a j s)").bitcast(F32).rearrange("p (n s) -> p n s", n=4)
        half_mix = pt_f32[:, 0:2, :]
        mixed = pt_f32[:, 2:4, :]
        out_sb = xnT

        psum = ctx.enter_context(nc.psum_tensor("psum", [P, 8, 512], F32))
        turn_bank = lambda j: psum[:, j % 2, :]
        QV_BANK, KO_BANK = psum[:, 2, :], psum[:, 3, :]
        row_bank = lambda t: psum[:, 4 + t, :]
        NORM_BANK = psum[:, 4, 0:4]
        gate_bank = lambda c: psum[:, (2, 6)[c % 2], :]
        up_bank = lambda c: psum[:, (3, 7)[c % 2], :]
        down_bank = lambda t: psum[:, 4 + t % 2, :]
        LAST_O_BANK = psum[:, 4, :]
        last_wo_bank = lambda t: psum[:, (5, 4)[t % 2], :]

        x_loaded = [sem(f"x_loaded{t}") for t in range(TT)]
        w_loaded = [sem(f"w_loaded{n}") for n in range(3)]
        wqkv_loaded = sem("wqkv_loaded")
        wo_loaded = sem("wo_loaded")
        bqkv_loaded = sem("bqkv_loaded")
        rows_loaded = sem("rows_loaded")
        scales_loaded = sem("scales_loaded")
        out_stored = [sem(f"out_stored{t}") for t in range(TT)]
        identity_made = sem("identity_made")
        ones_made = sem("ones_made")
        bias_made = sem("bias_made")
        squares_made = sem("squares_made")
        norms_full = sem("norms_full")
        norm_step = sem("norm_step")
        wqkv_hi_made = sem("wqkv_hi_made")
        wqkv_lo_made = sem("wqkv_lo_made")
        wo_hi_made = sem("wo_hi_made")
        wo_lo_made = sem("wo_lo_made")
        gu_scale_made = sem("gu_scale_made")
        scales_made = sem("scales_made")
        rows_made = sem("rows_made")
        w_cast = sem("w_cast")
        ln_step = sem("ln_step")
        xn_made = sem("xn_made")
        xt_full = sem("xt_full")
        xt_read = sem("xt_read")
        xhi_made = sem("xhi_made")
        xlo_made = sem("xlo_made")
        q_full = sem("q_full")
        k_full = sem("k_full")
        v_full = sem("v_full")
        q_read = sem("q_read")
        k_read = sem("k_read")
        v_read = sem("v_read")
        qkv_hi_made = sem("qkv_hi_made")
        qkv_lo_made = sem("qkv_lo_made")
        scores_full = sem("scores_full")
        max_made = sem("max_made")
        negmax_made = sem("negmax_made")
        exp_made = sem("exp_made")
        inv_made = sem("inv_made")
        probs_made = sem("probs_made")
        pt_full = sem("pt_full")
        pt_hi_made = sem("pt_hi_made")
        pt_lo_made = sem("pt_lo_made")
        o_full = sem("o_full")
        o_read = sem("o_read")
        o_hi_made = sem("o_hi_made")
        o_lo_made = sem("o_lo_made")
        wo_full = sem("wo_full")
        attn_read = sem("attn_read")
        attn_made = sem("attn_made")
        gu_full = sem("gu_full")
        gtanh_made = sem("gtanh_made")
        gact_made = sem("gact_made")
        hidden_made = sem("hidden_made")
        hi_made = sem("hi_made")
        lo_made = sem("lo_made")
        down_full = sem("down_full")
        halfy_made = sem("halfy_made")
        ytanh_made = sem("ytanh_made")
        halfmix_made = sem("halfmix_made")
        mixed_made = sem("mixed_made")
        out_made = sem("out_made")

        x_tiles = x.rearrange("b (t p) h -> b t p h", p=P)
        out_tiles = out.rearrange("b (t p) h -> b t p h", p=P)
        gate_rows = gate_t.rearrange("(c p) f -> c p f", p=P)
        up_rows = up_t.rearrange("(c p) f -> c p f", p=P)

        block = ctx.enter_context(nc.Block())

        @block.sync
        def _(sp):
            def load_x(b, t):
                sp.dma_start(x_sb[:, t, :], x_tiles[b, t]).then_inc(x_loaded[t], 16)

            def load_w(b, n):
                if b >= 1:
                    sp.wait_ge(w_cast, (b - 1) * 3 + (n + 1))
                sp.dma_start(w_stage[:, n, :], (gate_rows, up_rows, down_t)[n][b]).then_inc(w_loaded[n], 16)

            def reload_x(b):
                for t in range(TT):
                    sp.wait_ge(xn_made, (b - 1) * TT + (t + 1))
                    load_x(b, t)

            for t in range(TT):
                load_x(0, t)
            sp.dma_start(wqkv_sb[:], wqkv.rearrange("(c p) f -> p c f", p=P)).then_inc(wqkv_loaded, 16)
            sp.dma_start(wo_sb[:], wo).then_inc(wo_loaded, 16)
            reload_x(1)
            for n in range(3):
                load_w(0, n)
            sp.dma_start(bo_row[:], bo.to_broadcast([P, H])).then_inc(rows_loaded, 16)
            sp.dma_start(half_down_s[:], down_s.to_broadcast([P, H])).then_inc(rows_loaded, 16)
            reload_x(2)
            load_w(1, 0)
            load_w(1, 1)
            load_w(1, 2)
            load_w(2, 0)
            load_w(2, 1)
            reload_x(3)
            load_w(2, 2)
            for n in range(3):
                load_w(3, n)

            sp.wait_ge(xn_made, B * TT)
            for t in range(TT):
                load_x(0, t)

            def store_group(i):
                for t in range(TT):
                    sp.wait_ge(out_made, i * TT + (t + 1))
                    sp.dma_start(out_tiles[i, t], out_sb[:, t, :]).then_inc(out_stored[t], 16)

            with sp.Fori(0, B - 1) as i:
                store_group(i)
                for t in range(TT):
                    sp.wait_ge(out_stored[t], (i + 1) * 16)
                    load_x(i + 1, t)
            store_group(B - 1)
            for t in range(TT):
                sp.wait_ge(out_stored[t], B * 16)

        @block.gpsimd
        def _(pool):
            nc.gpsimd.memset(identity[:], 0.0).then_inc(identity_made, 1)
            nc.gpsimd.memset(ones[:], 1.0).then_inc(ones_made, 1)
            pool.wait_ge(identity_made, 1)
            nc.gpsimd.affine_select(out=identity[:], in_=identity[:], compare_op=ALU.not_equal, fill=1.0,
                                    base=0, pattern=[[-1, P]], channel_multiplier=1).then_inc(identity_made, 1)

            def take_xn_lo(b):
                for j in range(HC):
                    pool.wait_ge(xhi_made, b * HC + (j + 1))
                    nc.gpsimd.tensor_tensor(xn_lo[:, b, j, :], xnT[:, j, :], xn_hi[:, b, j, :],
                                            ALU.subtract).then_inc(xlo_made, 1)

            def take_qkv_lo(b):
                for n in range(3):
                    pool.wait_ge(qkv_hi_made, b * 3 + (n + 1))
                    nc.gpsimd.tensor_tensor(qkv_lo[:, n, :], qkv_f32[:, n, :], qkv_hi[:, n, :],
                                            ALU.subtract).then_inc(qkv_lo_made, 1)

            def add_bo(b):
                for t in range(TT):
                    pool.wait_ge(attn_read, b * TT + (t + 1) + PRIMED)
                    nc.gpsimd.tensor_tensor(attn[:, b, t, :], attn[:, b, t, :], bo_row[:],
                                            ALU.add).then_inc(attn_made, 1)

            take_xn_lo(0)
            take_qkv_lo(0)
            pool.wait_ge(rows_loaded, 32)
            with pool.Fori(0, B - 1) as b:
                take_xn_lo(b + 1)
                take_qkv_lo(b + 1)
                add_bo(b)

            def take_hidden_lo(i, c):
                pool.wait_ge(hi_made, i * FC + (c + 1))
                nc.gpsimd.tensor_tensor(hid_lo[:, c, :], hidden[:, c % 2, :], hid_hi[:, c, :],
                                        ALU.subtract).then_inc(lo_made, 1)

            for c in range(FC):
                take_hidden_lo(0, c)
                if c == 7:
                    add_bo(B - 1)
            with pool.Fori(1, B) as i:
                for c in range(FC):
                    take_hidden_lo(i, c)

        @block.scalar
        def _(act):
            def evacuate_xt(b, first=False):
                for j in range(HC):
                    act.wait_ge(xt_full, b * HC + (j + 1))
                    if j == 0 and not first:
                        act.wait_ge(xlo_made, b * HC)
                    nc.scalar.activation(xnT[:, j, :], turn_bank(j), ACT.Copy).then_inc(xt_read, 1)

            def evacuate_q(b, first=False):
                act.wait_ge(q_full, b + 1)
                if not first:
                    act.wait_ge(qkv_lo_made, b * 3)
                nc.scalar.activation(qkv_f32[:, 0, :], QV_BANK, ACT.Identity, bias=bias[:, 0:1],
                                     scale=QKV_SCALE / XN_SCALE).then_inc(q_read, 1)

            def evacuate_k(b):
                act.wait_ge(k_full, b + 1)
                nc.scalar.activation(qkv_f32[:, 1, :], KO_BANK, ACT.Identity, bias=bias[:, 1:2],
                                     scale=QKV_SCALE / XN_SCALE).then_inc(k_read, 1)

            def evacuate_v(b):
                act.wait_ge(v_full, b + 1)
                nc.scalar.activation(qkv_f32[:, 2, :], QV_BANK, ACT.Copy,
                                     scale=QKV_SCALE / XN_SCALE).then_inc(v_read, 1)

            def exponentials(b):
                for t in range(TT):
                    act.wait_ge(negmax_made, b * TT + (t + 1))
                    nc.scalar.activation(probs[:, t, :], row_bank(t), ACT.Exp, bias=neg_max[:, t:t + 1],
                                         scale=score_scale[:], accum_out=row_sum[:, t:t + 1]).then_inc(exp_made, 1)

            def take_pt_hi(b, chunks):
                for j in chunks:
                    act.wait_ge(pt_full, b * TT + (j + 1))
                    nc.scalar.activation(pt_hi[:, j, :], turn_bank(j), ACT.Copy).then_inc(pt_hi_made, 1)

            def evacuate_o(b, bank):
                act.wait_ge(o_full, b + 1)
                nc.scalar.activation(o_f32[:], bank, ACT.Identity, bias=bias[:, 2:3],
                                     scale=1.0 / PROBS_SCALE).then_inc(o_read, 1)

            def turn_weights(b, n):
                act.wait_ge(w_loaded[n], (b + 1) * 16)
                dst, src = (gate_w, up_w)[n % 2][:, b, :], w_stage[:, n, :]
                if n == 2:
                    dst, src = down_w[:, :, bass.ts(b, H // B)], src.rearrange("p (c h) -> p c h", c=FC)
                nc.scalar.activation(dst, src, ACT.Copy).then_inc(w_cast, 1)

            def evacuate_attn(b, tiles, bank):
                for t in tiles:
                    act.wait_ge(wo_full, b * TT + (t + 1))
                    nc.scalar.activation(attn[:, b, t, :], bank(t), ACT.Copy,
                                         scale=attn_scale[:]).then_inc(attn_read, 1)

            def gate_chunk(i, c):
                act.wait_ge(gu_full, i * FC + (c + 1))
                nc.scalar.activation(gate_tanh[:, c % 2, :], gate_bank(c), ACT.Tanh,
                                     scale=tanh_scale[:, c:c + 1]).then_inc(gtanh_made, 1)
                act.wait_ge(hidden_made, i * FC + (c + 1))
                nc.scalar.activation(hid_hi[:, c, :], hidden[:, c % 2, :], ACT.Copy).then_inc(hi_made, 1)

            def finish_group(i):
                for t in range(TT):
                    act.wait_ge(halfy_made, i * TT + (t + 1))
                    nc.scalar.activation(y_tanh[:, t % 2, :], half_y[:, t % 2, :],
                                         ACT.Tanh).then_inc(ytanh_made, 1)

            act.dma_start(gate_s_sb[:], gate_s).then_inc(scales_loaded, 16)
            act.dma_start(up_s_sb[:], up_s).then_inc(scales_loaded, 16)
            act.dma_start(bqkv_sb[:], bqkv).then_inc(bqkv_loaded, 16)

            act.sem_inc(attn_read, PRIMED)
            junk = probs[:].rearrange("p t s -> p (t s)")
            act.wait_ge(wqkv_loaded, 16)
            nc.scalar.activation(junk[:, 0:3 * H], wqkv_sb[:].rearrange("p c f -> p (c f)"), ACT.Square,
                                 accum_out=square_parts[:, 0:1]).then_inc(squares_made, 1)
            act.wait_ge(wo_loaded, 16)
            nc.scalar.activation(junk[:, 3 * H:4 * H], wo_sb[:], ACT.Square,
                                 accum_out=square_parts[:, 1:2]).then_inc(squares_made, 1)
            act.wait_ge(bqkv_loaded, 16)
            nc.scalar.activation(qkv_hi[:, 0, 0:3], bqkv_sb[:], ACT.Square, scale=QKV_SCALE,
                                 accum_out=square_parts[:, 3:4]).then_inc(squares_made, 1)
            act.wait_ge(gu_scale_made, 1)
            nc.scalar.activation(qkv_hi[:, 1, 0:FC], gu_scale[:], ACT.Square,
                                 accum_out=square_parts[:, 2:3]).then_inc(squares_made, 1)
            evacuate_xt(0, first=True)
            act.wait_ge(norm_step, NORM_STEPS)
            for n in range(3):
                nc.scalar.activation(wqkv_hi[:, :, bass.ts(n, D)], wqkv_sb[:, :, bass.ts(n, D)], ACT.Copy,
                                     scale=w_scale[:, 0:1]).then_inc(wqkv_hi_made, 1)
            nc.scalar.activation(wo_hi[:], wo_sb[:], ACT.Copy, scale=w_scale[:, 1:2]).then_inc(wo_hi_made, 1)
            act.wait_ge(bias_made, 1)
            act.wait_ge(wqkv_lo_made, 3)
            evacuate_q(0, first=True)
            evacuate_k(0)
            turn_weights(0, 0)
            evacuate_v(0)
            turn_weights(0, 1)
            act.wait_ge(wo_lo_made, 1)
            act.wait_ge(norm_step, NORM_STEPS + 2)
            with act.Fori(0, B - 1) as b:
                evacuate_xt(b + 1)
                exponentials(b)
                turn_weights(b, 2)
                evacuate_q(b + 1)
                evacuate_k(b + 1)
                take_pt_hi(b, range(TT))
                turn_weights(b + 1, 0)
                evacuate_o(b, KO_BANK)
                evacuate_v(b + 1)
                turn_weights(b + 1, 1)
                evacuate_attn(b, range(TT), row_bank)
            exponentials(B - 1)
            turn_weights(B - 1, 2)
            act.wait_ge(w_cast, 3 * B)
            act.wait_ge(scales_made, 2)
            gate_chunk(0, 0)
            gate_chunk(0, 1)
            take_pt_hi(B - 1, range(0, 2))
            gate_chunk(0, 2)
            take_pt_hi(B - 1, range(2, TT))
            gate_chunk(0, 3)
            evacuate_o(B - 1, LAST_O_BANK)
            gate_chunk(0, 4)
            evacuate_attn(B - 1, range(0, 2), last_wo_bank)
            gate_chunk(0, 5)
            evacuate_attn(B - 1, range(2, TT), last_wo_bank)
            for c in range(6, FC):
                gate_chunk(0, c)
            finish_group(0)
            with act.Fori(1, B) as i:
                for c in range(FC):
                    gate_chunk(i, c)
                finish_group(i)

        @block.vector
        def _(dve):
            LN_STEPS = 16

            def layernorm_stats(b):
                for t in range(TT):
                    dve.wait_ge(x_loaded[t], (b + 1) * 16)
                    last = nc.vector.bn_stats(stats[:, t, :], x_sb[:, t, :])
                last.then_inc(ln_step, 1)

            def layernorm_variance(b):
                mean_e, mean_o = stats[:, :, 1], stats[:, :, 4]
                dve.wait_ge(ln_step, b * LN_STEPS + 1)
                nc.vector.tensor_tensor(mean_gap[:], mean_e, mean_o, ALU.subtract)
                nc.vector.tensor_tensor(mean_sum[:], mean_e, mean_o, ALU.add)
                nc.vector.tensor_tensor(square_sum[:], stats[:, :, 2], stats[:, :, 5], ALU.add).then_inc(ln_step, 1)
                dve.wait_ge(ln_step, b * LN_STEPS + 2)
                nc.vector.scalar_tensor_tensor(out=gap_square[:], in0=mean_gap[:], scalar=0.25, in1=mean_gap[:],
                                               op0=ALU.mult, op1=ALU.mult)
                nc.vector.tensor_scalar(mean[:], mean_sum[:], 0.5, None, ALU.mult)
                nc.vector.tensor_scalar(var[:], square_sum[:], 1.0 / H, EPS, ALU.mult, ALU.add).then_inc(ln_step, 1)
                dve.wait_ge(ln_step, b * LN_STEPS + 3)
                nc.vector.tensor_tensor(var_eps[:], var[:], gap_square[:], ALU.add).then_inc(ln_step, 1)
                dve.wait_ge(ln_step, b * LN_STEPS + 4)
                nc.vector.tensor_scalar(rs_bits[:], var_eps[:].bitcast(I32), 1, None,
                                        ALU.logical_shift_right).then_inc(ln_step, 1)
                dve.wait_ge(ln_step, b * LN_STEPS + 5)
                nc.vector.tensor_scalar(rs_y[:, 0, :].bitcast(I32), rs_bits[:], -1.0, float(RSQRT_MAGIC),
                                        ALU.mult, ALU.add).then_inc(ln_step, 1)

            def layernorm_newton(b):
                for k in range(3):
                    dve.wait_ge(ln_step, b * LN_STEPS + (6 + 3 * k))
                    nc.vector.tensor_tensor(rs_t[:, k, :], rs_y[:, k, :], rs_y[:, k, :],
                                            ALU.mult).then_inc(ln_step, 1)
                    dve.wait_ge(ln_step, b * LN_STEPS + (7 + 3 * k))
                    nc.vector.scalar_tensor_tensor(out=rs_u[:, k, :], in0=rs_t[:, k, :], scalar=-0.5,
                                                   in1=var_eps[:], op0=ALU.mult, op1=ALU.mult).then_inc(ln_step, 1)
                    dve.wait_ge(ln_step, b * LN_STEPS + (8 + 3 * k))
                    nc.vector.scalar_tensor_tensor(out=rs_y[:, k + 1, :], in0=rs_u[:, k, :], scalar=1.5,
                                                   in1=rs_y[:, k, :], op0=ALU.add, op1=ALU.mult).then_inc(ln_step, 1)
                dve.wait_ge(ln_step, b * LN_STEPS + 15)
                nc.vector.tensor_scalar(rstd[:], rs_y[:, 3, :], XN_SCALE, None, ALU.mult).then_inc(ln_step, 1)

            def layernorm_apply(b, first=False):
                dve.wait_ge(ln_step, (b + 1) * LN_STEPS)
                if not first:
                    dve.wait_ge(xt_full, b * HC)
                for t in range(TT):
                    nc.vector.tensor_scalar(xn[:, t, :], x_sb[:, t, :], mean[:, t:t + 1], rstd[:, t:t + 1],
                                            ALU.subtract, ALU.mult).then_inc(xn_made, 1)

            def take_xn_hi(b):
                for j in range(HC):
                    dve.wait_ge(xt_read, b * HC + (j + 1))
                    nc.vector.tensor_copy(xn_hi[:, b, j, :], xnT[:, j, :]).then_inc(xhi_made, 1)

            def take_qkv_hi(b, n):
                dve.wait_ge((q_read, k_read, v_read)[n], b + 1)
                nc.vector.tensor_copy(qkv_hi[:, n, :], qkv_f32[:, n, :]).then_inc(qkv_hi_made, 1)

            def row_maximum(b, t):
                dve.wait_ge(scores_full, b * TT + (t + 1))
                nc.vector.reduce_max(row_max[:, t:t + 1], row_bank(t), AX_X).then_inc(max_made, 1)

            def negate_maximum(b, t):
                dve.wait_ge(max_made, b * TT + (t + 1))
                nc.vector.tensor_scalar(neg_max[:, t:t + 1], row_max[:, t:t + 1], neg_score_scale[:], None,
                                        ALU.mult).then_inc(negmax_made, 1)

            def invert_sum(b, t):
                dve.wait_ge(exp_made, b * TT + (t + 1))
                nc.vector.reciprocal(inv_sum[:, t:t + 1], row_sum[:, t:t + 1]).then_inc(inv_made, 1)

            def normalize(b, t):
                dve.wait_ge(inv_made, b * TT + (t + 1))
                nc.vector.tensor_scalar(probs[:, t, :], probs[:, t, :], inv_sum[:, t:t + 1], PROBS_SCALE,
                                        ALU.mult, ALU.mult).then_inc(probs_made, 1)

            def softmax(b):
                row_maximum(b, 0)
                negate_maximum(b, 0)
                row_maximum(b, 1)
                row_maximum(b, 2)
                negate_maximum(b, 1)
                invert_sum(b, 0)
                negate_maximum(b, 2)
                row_maximum(b, 3)
                normalize(b, 0)
                negate_maximum(b, 3)
                invert_sum(b, 1)
                invert_sum(b, 2)
                normalize(b, 1)
                normalize(b, 2)
                invert_sum(b, 3)
                normalize(b, 3)

            def take_pt_lo(b, chunks):
                for j in chunks:
                    dve.wait_ge(pt_hi_made, b * TT + (j + 1))
                    nc.vector.tensor_tensor(pt_lo[:, j, :], turn_bank(j), pt_hi[:, j, :],
                                            ALU.subtract).then_inc(pt_lo_made, 1)

            def split_o(b):
                dve.wait_ge(o_read, b + 1)
                nc.vector.tensor_copy(oT_hi[:], o_f32[:]).then_inc(o_hi_made, 1)
                dve.wait_ge(o_hi_made, b + 1)
                nc.vector.tensor_tensor(oT_lo[:], o_f32[:], oT_hi[:], ALU.subtract).then_inc(o_lo_made, 1)

            def attend(b, with_layernorm):
                take_xn_hi(b + 1)
                softmax(b)
                take_qkv_hi(b + 1, 0)
                if with_layernorm:
                    layernorm_stats(b + 2)
                take_qkv_hi(b + 1, 1)
                take_pt_lo(b, range(0, 2))
                if with_layernorm:
                    layernorm_variance(b + 2)
                take_pt_lo(b, range(2, TT))
                if with_layernorm:
                    layernorm_newton(b + 2)
                split_o(b)
                take_qkv_hi(b + 1, 2)
                if with_layernorm:
                    layernorm_apply(b + 2)

            def gate_chunk(i, c):
                dve.wait_ge(gtanh_made, i * FC + (c + 1))
                nc.vector.scalar_tensor_tensor(out=gate_act[:, c % 2, :], in0=gate_tanh[:, c % 2, :], scalar=1.0,
                                               in1=gate_bank(c), op0=ALU.add, op1=ALU.mult).then_inc(gact_made, 1)
                dve.wait_ge(gact_made, i * FC + (c + 1))
                if c >= 2:
                    dve.wait_ge(lo_made, i * FC + (c - 1))
                nc.vector.scalar_tensor_tensor(out=hidden[:, c % 2, :], in0=gate_act[:, c % 2, :],
                                               scalar=hid_scale[:, c:c + 1], in1=up_bank(c),
                                               op0=ALU.mult, op1=ALU.mult).then_inc(hidden_made, 1)

            def finish_group(i):
                for t in range(TT):
                    dve.wait_ge(down_full, i * TT + (t + 1))
                    if t >= 2:
                        dve.wait_ge(mixed_made, i * TT + (t - 1))
                    nc.vector.tensor_tensor(half_y[:, t % 2, :], down_bank(t), half_down_s[:],
                                            ALU.mult).then_inc(halfy_made, 1)
                    dve.wait_ge(halfy_made, i * TT + (t + 1))
                    dve.wait_ge(attn_made, (i + 1) * TT)
                    nc.vector.tensor_tensor(half_mix[:, t % 2, :], half_y[:, t % 2, :], attn[:, i, t, :],
                                            ALU.mult).then_inc(halfmix_made, 1)
                    dve.wait_ge(ytanh_made, i * TT + (t + 1))
                    dve.wait_ge(halfmix_made, i * TT + (t + 1))
                    nc.vector.scalar_tensor_tensor(out=mixed[:, t % 2, :], in0=y_tanh[:, t % 2, :], scalar=1.0,
                                                   in1=half_mix[:, t % 2, :], op0=ALU.add,
                                                   op1=ALU.mult).then_inc(mixed_made, 1)
                    dve.wait_ge(mixed_made, i * TT + (t + 1))
                    dve.wait_ge(x_loaded[t], (i + (B + 1)) * 16)
                    nc.vector.tensor_tensor(out_sb[:, t, :], mixed[:, t % 2, :], x_sb[:, t, :],
                                            ALU.add).then_inc(out_made, 1)

            dve.wait_ge(scales_loaded, 32)
            nc.vector.tensor_tensor(gu_scale[:], gate_s_sb[:], up_s_sb[:], ALU.mult).then_inc(gu_scale_made, 1)
            layernorm_stats(0)
            layernorm_variance(0)
            layernorm_newton(0)
            layernorm_apply(0, first=True)

            dve.wait_ge(norms_full, 1)
            nc.vector.tensor_copy(square_sums[:], NORM_BANK).then_inc(norm_step, 1)
            dve.wait_ge(norm_step, 1)
            nc.vector.tensor_tensor(norm_square[:, 0:1], square_sums[:, 0:1], square_sums[:, 3:4], ALU.add)
            nc.vector.tensor_copy(norm_square[:, 1:3], square_sums[:, 1:3]).then_inc(norm_step, 1)
            dve.wait_ge(norm_step, 2)
            nc.vector.tensor_scalar(norm_bits[:], norm_square[:].bitcast(I32), 1, None,
                                    ALU.logical_shift_right).then_inc(norm_step, 1)
            dve.wait_ge(norm_step, 3)
            nc.vector.tensor_scalar(norm_guess[:], norm_bits[:], -1.0, float(RSQRT_MAGIC),
                                    ALU.mult, ALU.add).then_inc(norm_step, 1)
            dve.wait_ge(norm_step, 4)
            nc.vector.tensor_scalar(norm_inverse[:].bitcast(I32), norm_guess[:], EXPONENT_BITS, None,
                                    ALU.bitwise_and).then_inc(norm_step, 1)
            dve.wait_ge(norm_step, 5)
            nc.vector.tensor_scalar(w_scale[:], norm_inverse[:], W_SCALE, None, ALU.mult).then_inc(norm_step, 1)
            dve.wait_ge(norm_step, NORM_STEPS)
            take_xn_hi(0)
            for n in range(3):
                dve.wait_ge(wqkv_hi_made, n + 1)
                nc.vector.scalar_tensor_tensor(out=wqkv_lo[:, :, bass.ts(n, D)], in0=wqkv_sb[:, :, bass.ts(n, D)],
                                               scalar=w_scale[:, 0:1], in1=wqkv_hi[:, :, bass.ts(n, D)],
                                               op0=ALU.mult, op1=ALU.subtract).then_inc(wqkv_lo_made, 1)
            nc.vector.tensor_scalar(w_unscale[:].bitcast(I32), w_scale[:].bitcast(I32), -1.0, float(0x7F000000),
                                    ALU.mult, ALU.add).then_inc(norm_step, 1)
            nc.vector.tensor_scalar(bias[:], bqkv_sb[:], w_scale[:, 0:1], QKV_SCALE, ALU.mult,
                                    ALU.mult).then_inc(bias_made, 1)
            dve.wait_ge(wo_hi_made, 1)
            nc.vector.scalar_tensor_tensor(out=wo_lo[:], in0=wo_sb[:], scalar=w_scale[:, 1:2], in1=wo_hi[:],
                                           op0=ALU.mult, op1=ALU.subtract).then_inc(wo_lo_made, 1)
            dve.wait_ge(norm_step, NORM_STEPS + 1)
            nc.vector.tensor_scalar(score_scale[:], w_unscale[:, 0:1], w_unscale[:, 0:1],
                                    SM_SCALE / QKV_SCALE / QKV_SCALE, ALU.mult, ALU.mult)
            nc.vector.tensor_scalar(neg_score_scale[:], w_unscale[:, 0:1], w_unscale[:, 0:1],
                                    -SM_SCALE / QKV_SCALE / QKV_SCALE, ALU.mult, ALU.mult)
            nc.vector.tensor_scalar(attn_scale[:], w_unscale[:, 0:1], w_unscale[:, 1:2], 1.0 / QKV_SCALE,
                                    ALU.mult, ALU.mult).then_inc(norm_step, 1)
            layernorm_stats(1)
            layernorm_variance(1)
            layernorm_newton(1)
            take_qkv_hi(0, 0)
            take_qkv_hi(0, 1)
            layernorm_apply(1)

            nc.vector.tensor_scalar(tanh_scale[:], gate_s_sb[:], 0.5 / XN_SCALE, None,
                                    ALU.mult).then_inc(scales_made, 1)
            nc.vector.tensor_scalar(hid_scale[:], gu_scale[:], w_scale[:, 2:3],
                                    0.5 * HID_SCALE / XN_SCALE / XN_SCALE, ALU.mult,
                                    ALU.mult).then_inc(scales_made, 1)
            take_qkv_hi(0, 2)
            dve.wait_ge(rows_loaded, 32)
            nc.vector.tensor_scalar(half_down_s[:], half_down_s[:], w_unscale[:, 2:3], 0.5 / HID_SCALE, ALU.mult,
                                    ALU.mult).then_inc(rows_made, 1)
            dve.wait_ge(norm_step, NORM_STEPS + 2)
            dve.wait_ge(scales_made, 2)
            dve.wait_ge(rows_made, 1)

            with dve.Fori(0, B - 2) as b:
                attend(b, True)
            attend(B - 2, False)

            softmax(B - 1)
            gate_chunk(0, 0)
            gate_chunk(0, 1)
            take_pt_lo(B - 1, range(0, 2))
            gate_chunk(0, 2)
            take_pt_lo(B - 1, range(2, TT))
            gate_chunk(0, 3)
            split_o(B - 1)
            for c in range(4, FC):
                gate_chunk(0, c)
            finish_group(0)
            with dve.Fori(1, B) as i:
                for c in range(FC):
                    gate_chunk(i, c)
                finish_group(i)

        @block.tensor
        def _(pe):
            def products(out, terms):
                for n, (stationary, moving) in enumerate(terms):
                    last = nc.tensor.matmul(out, stationary, moving, start=(n == 0), stop=(n == len(terms) - 1))
                return last

            def transpose_xn(b):
                for j in range(HC):
                    if j >= 2:
                        pe.wait_ge(xt_read, b * HC + (j - 1))
                    for t in range(TT):
                        if j == 0:
                            pe.wait_ge(xn_made, b * TT + (t + 1))
                        last = nc.tensor.transpose(turn_bank(j)[:, bass.ts(t, P)], xn[:, t, bass.ts(j, P)],
                                                   identity[:])
                    last.then_inc(xt_full, 1)

            def project_q_or_k(b, n, bank, full):
                cols = bass.ts(n, D)
                for j in range(HC):
                    if n == 0:
                        pe.wait_ge(xhi_made, b * HC + (j + 1))
                    nc.tensor.matmul(bank, wqkv_hi[:, j, cols], xn_hi[:, b, j, :], start=(j == 0), stop=False)
                    nc.tensor.matmul(bank, wqkv_lo[:, j, cols], xn_hi[:, b, j, :], start=False, stop=False)
                for j in range(HC):
                    if n == 0:
                        pe.wait_ge(xlo_made, b * HC + (j + 1))
                    last = nc.tensor.matmul(bank, wqkv_hi[:, j, cols], xn_lo[:, b, j, :], start=False,
                                            stop=(j == HC - 1))
                last.then_inc(full, 1)

            def project_q(b, first=False):
                if not first:
                    pe.wait_ge(v_read, b)
                project_q_or_k(b, 0, QV_BANK, q_full)

            def project_k(b):
                project_q_or_k(b, 1, KO_BANK, k_full)

            def project_v(b, tiles):
                cols = bass.ts(2, D)
                for t in tiles:
                    if t == 0:
                        pe.wait_ge(q_read, b + 1)
                    rows = bass.ts(t, P)
                    last = products(QV_BANK[:, bass.ts(t, D)],
                                    [(half[:, b, j, rows], w[:, j, cols]) for j in range(HC)
                                     for half, w in ((xn_hi, wqkv_hi), (xn_hi, wqkv_lo), (xn_lo, wqkv_hi))])
                    if t == TT - 1:
                        last.then_inc(v_full, 1)

            def scores(b):
                pe.wait_ge(qkv_lo_made, b * 3 + 2)
                pe.wait_ge(attn_read, b * TT + PRIMED)
                for t in range(TT):
                    cols = bass.ts(t, P)
                    products(row_bank(t), [(qkv_hi[:, 0, cols], qkv_hi[:, 1, :]), (qkv_hi[:, 0, cols], qkv_lo[:, 1, :]),
                                           (qkv_lo[:, 0, cols], qkv_hi[:, 1, :])]).then_inc(scores_full, 1)

            def transpose_probs(b, chunks):
                for j in chunks:
                    if j >= 2:
                        pe.wait_ge(pt_lo_made, b * TT + (j - 1))
                    for t in range(TT):
                        if j == 0:
                            pe.wait_ge(probs_made, b * TT + (t + 1))
                        last = nc.tensor.transpose(turn_bank(j)[:, bass.ts(t, P)], probs[:, t, bass.ts(j, P)],
                                                   identity[:])
                    last.then_inc(pt_full, 1)

            def probs_times_v(b, bank):
                pe.wait_ge(qkv_lo_made, (b + 1) * 3)
                for j in range(TT):
                    cols = bass.ts(j, D)
                    pe.wait_ge(pt_hi_made, b * TT + (j + 1))
                    nc.tensor.matmul(bank, qkv_hi[:, 2, cols], pt_hi[:, j, :], start=(j == 0), stop=False)
                    nc.tensor.matmul(bank, qkv_lo[:, 2, cols], pt_hi[:, j, :], start=False, stop=False)
                for j in range(TT):
                    cols = bass.ts(j, D)
                    pe.wait_ge(pt_lo_made, b * TT + (j + 1))
                    last = nc.tensor.matmul(bank, qkv_hi[:, 2, cols], pt_lo[:, j, :], start=False, stop=(j == TT - 1))
                last.then_inc(o_full, 1)

            def project_o(b, tiles, bank, bank_free):
                for t in tiles:
                    rows = bass.ts(t, P)
                    bank_free(t)
                    pe.wait_ge(o_hi_made, b + 1)
                    nc.tensor.matmul(bank(t), oT_hi[:, rows], wo_hi[:], start=True, stop=False)
                    nc.tensor.matmul(bank(t), oT_hi[:, rows], wo_lo[:], start=False, stop=False)
                    pe.wait_ge(o_lo_made, b + 1)
                    nc.tensor.matmul(bank(t), oT_lo[:, rows], wo_hi[:], start=False, stop=True).then_inc(wo_full, 1)

            def gate_chunk(i, c):
                if c >= 2:
                    pe.wait_ge(hidden_made, i * FC + (c - 1))
                for bank, w in ((gate_bank(c), gate_w), (up_bank(c), up_w)):
                    last = products(bank, [(w[:, j, bass.ts(c, P)], half[:, i, j, :])
                                           for j in range(HC) for half in (xn_hi, xn_lo)])
                last.then_inc(gu_full, 1)

            def down_group(i):
                for t in range(TT):
                    if t >= 2:
                        pe.wait_ge(halfy_made, i * TT + (t - 1))
                    for c in range(FC):
                        if t == 0:
                            pe.wait_ge(lo_made, i * FC + (c + 1))
                        for half in (hid_hi, hid_lo):
                            last = nc.tensor.matmul(down_bank(t), half[:, c, bass.ts(t, P)], down_w[:, c, :],
                                                    start=(c == 0 and half is hid_hi),
                                                    stop=(c == FC - 1 and half is hid_lo))
                    last.then_inc(down_full, 1)

            pe.wait_ge(ones_made, 1)
            pe.wait_ge(squares_made, 4)
            nc.tensor.matmul(NORM_BANK, ones[:], square_parts[:], start=True, stop=True).then_inc(norms_full, 1)
            pe.wait_ge(identity_made, 2)
            transpose_xn(0)
            pe.wait_ge(wqkv_lo_made, 1)
            project_q(0, first=True)
            pe.wait_ge(wqkv_lo_made, 3)
            project_k(0)
            project_v(0, range(TT))
            pe.wait_ge(wo_lo_made, 1)
            with pe.Fori(0, B - 1) as b:
                transpose_xn(b + 1)
                scores(b)
                project_q(b + 1)
                project_k(b + 1)
                transpose_probs(b, range(0, 2))
                project_v(b + 1, range(0, TT // 2))
                transpose_probs(b, range(2, TT))
                pe.wait_ge(k_read, b + 2)
                probs_times_v(b, KO_BANK)
                project_v(b + 1, range(TT // 2, TT))
                project_o(b, range(TT), row_bank, lambda t: None)

            scores(B - 1)
            pe.wait_ge(w_cast, 3 * B)
            pe.wait_ge(v_read, B)
            pe.wait_ge(o_read, B - 1)
            gate_chunk(0, 0)
            pe.wait_ge(exp_made, TT * B)
            gate_chunk(0, 1)
            transpose_probs(B - 1, range(0, 2))
            gate_chunk(0, 2)
            transpose_probs(B - 1, range(2, TT))
            gate_chunk(0, 3)
            probs_times_v(B - 1, LAST_O_BANK)
            gate_chunk(0, 4)

            def last_wo_free(t):
                if t >= 2:
                    pe.wait_ge(attn_read, TT * (B - 1) + (t - 1) + PRIMED)

            project_o(B - 1, range(0, 2), last_wo_bank, last_wo_free)
            gate_chunk(0, 5)
            project_o(B - 1, range(2, TT), last_wo_bank, last_wo_free)
            for c in range(6, FC):
                gate_chunk(0, c)
            pe.wait_ge(attn_read, TT * B + PRIMED)
            down_group(0)
            with pe.Fori(1, B) as i:
                for c in range(FC):
                    gate_chunk(i, c)
                down_group(i)


def kernel(**inputs):
    import numpy as np
    import concourse.bacc as bacc
    from concourse.bass_utils import run_bass_kernel_spmd

    a = {name.removeprefix("L0_"): np.asarray(value) for name, value in inputs.items()}
    B, S, H = a["attn_x"].shape
    FF = a["ffn_gate_t"].shape[0]
    arrays = {
        "x": a["attn_x"],
        "wqkv": a["attn_Wqkv"],
        "bqkv": a["attn_bqkv"].reshape(3, P).T,
        "wo": a["attn_Wo"],
        "bo": a["attn_bo"].reshape(1, H),
        "gate_t": a["ffn_gate_t"].T,
        "up_t": a["ffn_up_t"].T,
        "down_t": a["ffn_down_t"].reshape(B, H // B, FF // P, P).transpose(0, 3, 2, 1).reshape(B, P, FF),
        "gate_s": a["ffn_gate_s"].reshape(FF // P, P).T,
        "up_s": a["ffn_up_s"].reshape(FF // P, P).T,
        "down_s": a["ffn_down_s"].reshape(1, H),
    }
    nc = bacc.Bacc("TRN2", target_bir_lowering=False, num_devices=1)
    named, args = {}, []
    for name, value in arrays.items():
        value = np.ascontiguousarray(value)
        named[f"in_{name}"] = value
        args.append(nc.dram_tensor(f"in_{name}", value.shape, mybir.dt.from_np(value.dtype), kind="ExternalInput").ap())
    args.append(nc.dram_tensor("out_0", (B, S, H), F32, kind="ExternalOutput").ap())
    gated_attention_ffn(nc, *args)
    result = run_bass_kernel_spmd(nc, [named], core_ids=[0])
    return result.results[0]["out_0"]
```

```python
from contextlib import ExitStack

import concourse.bass as bass
from concourse import mybir

ALU = mybir.AluOpType
ACT = mybir.ActivationFunctionType
AX_X = mybir.AxisListType.X
F32 = mybir.dt.float32
F16 = mybir.dt.float16
BF16 = mybir.dt.bfloat16
I32 = mybir.dt.int32

P = 128
EPS = 1e-5
XN_SCALE = 2.0**10
W_SCALE = 2.0**14
QKV_SCALE = 2.0**-4
PROBS_SCALE = 2.0**14
HID_SCALE = 2.0**-17
EXPONENT_BITS = 0x7F800000
RSQRT_MAGIC = 0x5F3759DF


def gated_attention_ffn(nc, x, wqkv, bqkv, wo, bo, gate_t, up_t, down_t, gate_s, up_s, down_s, out):
    B, S, H = x.shape
    D = wo.shape[0]
    FF = gate_t.shape[1]
    TT = S // P
    HC = H // P
    FC = FF // P
    SM_SCALE = float(D) ** -0.5
    NORM_STEPS = 3
    PRIMED = 2
    HT = TT // 2
    WARM_UP = 28
    PIECES = [(t, 0, H) for t in range(TT - 1)] + [(TT - 1, 0, H // 2), (TT - 1, H // 2, H)]
    PC = len(PIECES)
    STORES = [16 * sum(t == piece[0] for piece in PIECES) for t in range(TT)]
    assert D == P and S == 512 and H == 512 and FF % P == 0 and HC == B and TT == 4

    with ExitStack() as ctx:
        def sb(name, shape, dt):
            return ctx.enter_context(nc.sbuf_tensor(name, shape, dt))

        def sem(name):
            return ctx.enter_context(nc.semaphore(name))

        wqkv_sb = sb("wqkv_sb", [P, HC, 3 * D], F32)
        wo_sb = sb("wo_sb", [P, H], F32)
        wqkv_hi = sb("wqkv_hi", [P, HC, 3 * D], F16)
        wqkv_lo = sb("wqkv_lo", [P, HC, 3 * D], F16)
        wo_hi = sb("wo_hi", [P, H], F16)
        wo_lo = sb("wo_lo", [P, H], F16)
        bqkv_sb = sb("bqkv_sb", [P, 3], F32)
        bias = sb("bias", [P, 3], F32)
        square_parts = sb("square_parts", [P, 5], F32)
        norm_guess = sb("norm_guess", [P, 3], I32)
        norm_inverse = sb("norm_inverse", [P, 3], F32)
        w_scale = sb("w_scale", [P, 3], F32)
        w_unscale = sb("w_unscale", [P, 3], F32)
        score_scale = sb("score_scale", [P, 1], F32)
        neg_score_scale = sb("neg_score_scale", [P, 1], F32)
        attn_scale = sb("attn_scale", [P, 1], F32)
        bo_row = sb("bo_row", [P, H], F32)
        half_down_s = sb("half_down_s", [P, H], F32)
        gate_s_sb = sb("gate_s_sb", [P, FC], F32)
        up_s_sb = sb("up_s_sb", [P, FC], F32)
        tanh_scale = sb("tanh_scale", [P, FC], F32)
        gu_scale = sb("gu_scale", [P, FC], F32)
        hid_scale = sb("hid_scale", [P, FC], F32)
        identity = sb("identity", [P, P], F32)
        ones = sb("ones", [P, P], F32)
        hid_sb = sb("hid_sb", [P, 2, FC, S], F16)
        hid_hi, hid_lo = hid_sb[:, 0], hid_sb[:, 1]
        w_stage = hid_sb[:].rearrange("p a c s -> p (a c s)").bitcast(I32)[:, 0:3 * FF].rearrange(
            "p (n f) -> p n f", n=3)
        gate_w = sb("gate_w", [P, HC, FF], F16)
        up_w = sb("up_w", [P, HC, FF], F16)
        down_w = sb("down_w", [P, FC, H], F16)
        xn_hi = sb("xn_hi", [P, B, HC, S], F16)
        xn_lo = sb("xn_lo", [P, B, HC, S], F16)
        attn = sb("attn", [P, B, TT, H], F32)
        x_sb = sb("x_sb", [P, TT, H], F32)
        xn = sb("xn", [P, TT, H], F32)
        xnT = sb("xnT", [P, HC, S], F32)
        stats = sb("stats", [P, TT, 6], F32)
        mean_sum = sb("mean_sum", [P, TT], F32)
        mean_gap = sb("mean_gap", [P, TT], F32)
        square_sum = sb("square_sum", [P, TT], F32)
        gap_square = sb("gap_square", [P, TT], F32)
        mean = sb("mean", [P, TT], F32)
        var = sb("var", [P, TT], F32)
        var_eps = sb("var_eps", [P, TT], F32)
        rs_y = sb("rs_y", [P, 3, TT], F32)
        rs_scaled = sb("rs_scaled", [P, TT], F32)
        rs_t = sb("rs_t", [P, 3, TT], F32)
        rs_u = sb("rs_u", [P, 3, TT], F32)
        rstd = sb("rstd", [P, TT], F32)
        qkv_f32 = wqkv_sb[:].rearrange("p c f -> p (c f)").rearrange("p (n s) -> p n s", n=3)
        o_f32 = wo_sb
        qkv_hi = sb("qkv_hi", [P, 3, S], F16)
        qkv_lo = sb("qkv_lo", [P, 3, S], F16)
        row_max = sb("row_max", [P, TT], F32)
        neg_max = sb("neg_max", [P, TT], F32)
        row_sum = sb("row_sum", [P, TT], F32)
        inv_sum = sb("inv_sum", [P, TT], F32)
        probs = sb("probs", [P, TT, S], F32)
        pt_sb = sb("pt_sb", [P, 2, TT, S], F16)
        pt_hi, pt_lo = pt_sb[:, 0], pt_sb[:, 1]
        oT_hi = sb("oT_hi", [P, S], F16)
        oT_lo = sb("oT_lo", [P, S], F16)
        gate_tanh = xn[:, 0:2, :]
        gate_act = xn[:, 2:4, :]
        hidden = qkv_f32[:, 0:2, :]
        half_y = probs[:, 0:2, :]
        y_tanh = probs[:, 2:4, :]
        pt_f32 = pt_sb[:].rearrange("p a j s -> p (a j s)").bitcast(F32).rearrange("p (n s) -> p n s", n=4)
        half_mix = pt_f32[:, 0:2, :]
        mixed = pt_f32[:, 2:4, :]
        out_sb = xnT

        psum = ctx.enter_context(nc.psum_tensor("psum", [P, 8, 512], F32))
        turn_bank = lambda j: psum[:, j % 2, :]
        QV_BANK, KO_BANK = psum[:, 2, :], psum[:, 3, :]
        row_bank = lambda t: psum[:, 4 + t, :]
        NORM_BANK = psum[:, 4, 0:3]
        WARM_BANK = psum[:, 5, 0:P]
        gate_bank = lambda c: psum[:, (2, 6)[c % 2], :]
        up_bank = lambda c: psum[:, (3, 7)[c % 2], :]
        down_bank = lambda n, lo, hi: psum[:, 4 + n % 2, lo:hi]
        LAST_O_BANK = psum[:, 4, :]
        last_wo_bank = lambda t: psum[:, (5, 4)[t % 2], :]

        x_loaded = [sem(f"x_loaded{t}") for t in range(TT)]
        w_loaded = [sem(f"w_loaded{n}") for n in range(3)]
        wqkv_loaded = [sem(f"wqkv_loaded{n}") for n in range(2)]
        wo_loaded = sem("wo_loaded")
        bqkv_loaded = sem("bqkv_loaded")
        rows_loaded = sem("rows_loaded")
        scales_loaded = sem("scales_loaded")
        out_stored = [sem(f"out_stored{t}") for t in range(TT)]
        identity_made = sem("identity_made")
        ones_made = sem("ones_made")
        bias_made = sem("bias_made")
        squares_made = sem("squares_made")
        norms_full = sem("norms_full")
        norm_step = sem("norm_step")
        wqkv_hi_made = sem("wqkv_hi_made")
        wqkv_lo_made = sem("wqkv_lo_made")
        wo_hi_made = sem("wo_hi_made")
        wo_lo_made = sem("wo_lo_made")
        gu_scale_made = sem("gu_scale_made")
        scales_made = sem("scales_made")
        rows_made = sem("rows_made")
        w_cast = sem("w_cast")
        ln_step = sem("ln_step")
        xn_made = sem("xn_made")
        xt_full = sem("xt_full")
        xt_read = sem("xt_read")
        xhi_made = sem("xhi_made")
        xlo_made = sem("xlo_made")
        q_full = sem("q_full")
        k_full = sem("k_full")
        v_full = sem("v_full")
        q_read = sem("q_read")
        k_read = sem("k_read")
        v_read = sem("v_read")
        qkv_hi_made = sem("qkv_hi_made")
        qkv_lo_made = sem("qkv_lo_made")
        scores_full = sem("scores_full")
        max_made = sem("max_made")
        negmax_made = sem("negmax_made")
        exp_made = sem("exp_made")
        inv_made = sem("inv_made")
        probs_made = sem("probs_made")
        pt_full = sem("pt_full")
        pt_hi_made = sem("pt_hi_made")
        pt_lo_made = sem("pt_lo_made")
        o_full = sem("o_full")
        o_read = sem("o_read")
        o_hi_made = sem("o_hi_made")
        o_lo_made = sem("o_lo_made")
        wo_full = sem("wo_full")
        attn_read = sem("attn_read")
        attn_made = sem("attn_made")
        attn_done = sem("attn_done")
        gu_full = sem("gu_full")
        gtanh_made = sem("gtanh_made")
        gact_made = sem("gact_made")
        hidden_made = sem("hidden_made")
        hi_made = sem("hi_made")
        lo_made = sem("lo_made")
        down_full = sem("down_full")
        halfy_made = sem("halfy_made")
        ytanh_made = sem("ytanh_made")
        halfmix_made = sem("halfmix_made")
        mixed_made = sem("mixed_made")
        out_made = sem("out_made")

        x_tiles = x.rearrange("b (t p) h -> b t p h", p=P)
        out_tiles = out.rearrange("b (t p) h -> b t p h", p=P)
        wqkv_rows = wqkv.rearrange("(c p) f -> p c f", p=P)
        gate_rows = gate_t.rearrange("(c p) f -> c p f", p=P)
        up_rows = up_t.rearrange("(c p) f -> c p f", p=P)

        block = ctx.enter_context(nc.Block())

        @block.sync
        def _(sp):
            def load_x(b, t):
                sp.dma_start(x_sb[:, t, :], x_tiles[b, t]).then_inc(x_loaded[t], 16)

            def load_w(b, n):
                if b >= 1:
                    sp.wait_ge(w_cast, (b - 1) * 3 + (n + 1))
                sp.dma_start(w_stage[:, n, :], (gate_rows, up_rows, down_t)[n][b]).then_inc(w_loaded[n], 16)

            def reload_x(b):
                for t in range(TT):
                    sp.wait_ge(xn_made, (b - 1) * TT + (t + 1))
                    load_x(b, t)

            for t in range(TT):
                load_x(0, t)
            for n in range(2):
                sp.dma_start(wqkv_sb[:, bass.ts(n, HC // 2)], wqkv_rows[:, bass.ts(n, HC // 2)]).then_inc(
                    wqkv_loaded[n], 16)
            sp.dma_start(wo_sb[:], wo).then_inc(wo_loaded, 16)
            reload_x(1)
            for n in range(3):
                load_w(0, n)
            sp.dma_start(bo_row[:], bo.to_broadcast([P, H])).then_inc(rows_loaded, 16)
            sp.dma_start(half_down_s[:], down_s.to_broadcast([P, H])).then_inc(rows_loaded, 16)
            reload_x(2)
            load_w(1, 0)
            load_w(1, 1)
            load_w(1, 2)
            load_w(2, 0)
            load_w(2, 1)
            reload_x(3)
            load_w(2, 2)
            for n in range(3):
                load_w(3, n)

            sp.wait_ge(xn_made, B * TT)
            for t in range(TT):
                load_x(0, t)

            def store_group(i):
                for n, (t, lo, hi) in enumerate(PIECES):
                    sp.wait_ge(out_made, i * PC + (n + 1))
                    sp.dma_start(out_tiles[i, t][:, lo:hi], out_sb[:, t, lo:hi]).then_inc(out_stored[t], 16)

            with sp.Fori(0, B - 1) as i:
                store_group(i)
                for t in range(TT):
                    sp.wait_ge(out_stored[t], (i + 1) * STORES[t])
                    load_x(i + 1, t)
            store_group(B - 1)
            for t in range(TT):
                sp.wait_ge(out_stored[t], B * STORES[t])

        @block.gpsimd
        def _(pool):
            nc.gpsimd.memset(identity[:], 0.0).then_inc(identity_made, 1)
            nc.gpsimd.memset(ones[:], 1.0).then_inc(ones_made, 1)
            pool.wait_ge(identity_made, 1)
            nc.gpsimd.affine_select(out=identity[:], in_=identity[:], compare_op=ALU.not_equal, fill=1.0,
                                    base=0, pattern=[[-1, P]], channel_multiplier=1).then_inc(identity_made, 1)

            def take_xn_lo(b):
                for j in range(HC):
                    pool.wait_ge(xhi_made, b * HC + (j + 1))
                    nc.gpsimd.tensor_tensor(xn_lo[:, b, j, :], xnT[:, j, :], xn_hi[:, b, j, :],
                                            ALU.subtract).then_inc(xlo_made, 1)

            def take_qkv_lo(b):
                for n in range(3):
                    pool.wait_ge(qkv_hi_made, b * 3 + (n + 1))
                    nc.gpsimd.tensor_tensor(qkv_lo[:, n, :], qkv_f32[:, n, :], qkv_hi[:, n, :],
                                            ALU.subtract).then_inc(qkv_lo_made, 1)

            def add_bo(b):
                for t in range(HT):
                    pool.wait_ge(attn_read, b * HT + (t + 1) + PRIMED)
                    nc.gpsimd.tensor_tensor(attn[:, b, t, :], attn[:, b, t, :], bo_row[:],
                                            ALU.add).then_inc(attn_made, 1)

            take_xn_lo(0)
            take_qkv_lo(0)
            pool.wait_ge(rows_loaded, 32)
            with pool.Fori(0, B - 1) as b:
                take_xn_lo(b + 1)
                take_qkv_lo(b + 1)
                add_bo(b)

            def take_hidden_lo(i, c):
                pool.wait_ge(hi_made, i * FC + (c + 1))
                nc.gpsimd.tensor_tensor(hid_lo[:, c, :], hidden[:, c % 2, :], hid_hi[:, c, :],
                                        ALU.subtract).then_inc(lo_made, 1)

            for c in range(FC):
                take_hidden_lo(0, c)
                if c == 7:
                    add_bo(B - 1)
            with pool.Fori(1, B) as i:
                for c in range(FC):
                    take_hidden_lo(i, c)

        @block.scalar
        def _(act):
            def evacuate_xt(b, chunks=range(HC), first=False):
                for j in chunks:
                    act.wait_ge(xt_full, b * HC + (j + 1))
                    if j == 0 and not first:
                        act.wait_ge(xlo_made, b * HC)
                    nc.scalar.activation(xnT[:, j, :], turn_bank(j), ACT.Copy).then_inc(xt_read, 1)

            def evacuate_q(b, first=False):
                act.wait_ge(q_full, b + 1)
                if not first:
                    act.wait_ge(qkv_lo_made, b * 3)
                nc.scalar.activation(qkv_f32[:, 0, :], QV_BANK, ACT.Identity, bias=bias[:, 0:1],
                                     scale=QKV_SCALE / XN_SCALE).then_inc(q_read, 1)

            def evacuate_k(b):
                act.wait_ge(k_full, b + 1)
                nc.scalar.activation(qkv_f32[:, 1, :], KO_BANK, ACT.Identity, bias=bias[:, 1:2],
                                     scale=QKV_SCALE / XN_SCALE).then_inc(k_read, 1)

            def evacuate_v(b):
                act.wait_ge(v_full, b + 1)
                nc.scalar.activation(qkv_f32[:, 2, :], QV_BANK, ACT.Copy,
                                     scale=QKV_SCALE / XN_SCALE).then_inc(v_read, 1)

            def exponentials(b):
                act.wait_ge(norm_step, NORM_STEPS + 2)
                for t in range(TT):
                    act.wait_ge(negmax_made, b * TT + (t + 1))
                    nc.scalar.activation(probs[:, t, :], row_bank(t), ACT.Exp, bias=neg_max[:, t:t + 1],
                                         scale=score_scale[:], accum_out=row_sum[:, t:t + 1]).then_inc(exp_made, 1)

            def take_pt_hi(b, chunks):
                for j in chunks:
                    act.wait_ge(pt_full, b * TT + (j + 1))
                    nc.scalar.activation(pt_hi[:, j, :], turn_bank(j), ACT.Copy).then_inc(pt_hi_made, 1)

            def evacuate_o(b, bank):
                act.wait_ge(o_full, b + 1)
                act.wait_ge(wo_lo_made, 1)
                nc.scalar.activation(o_f32[:], bank, ACT.Identity, bias=bias[:, 2:3],
                                     scale=1.0 / PROBS_SCALE).then_inc(o_read, 1)

            def turn_weights(b, n):
                act.wait_ge(w_loaded[n], (b + 1) * 16)
                dst, src = (gate_w, up_w)[n % 2][:, b, :], w_stage[:, n, :]
                if n == 2:
                    dst, src = down_w[:, :, bass.ts(b, H // B)], src.rearrange("p (c h) -> p c h", c=FC)
                nc.scalar.activation(dst, src, ACT.Copy).then_inc(w_cast, 1)

            def evacuate_attn(b, bank):
                for t in range(HT):
                    act.wait_ge(wo_full, b * TT + (t + 1))
                    nc.scalar.activation(attn[:, b, t, :], bank(t), ACT.Copy,
                                         scale=attn_scale[:]).then_inc(attn_read, 1)

            def gate_chunk(i, c):
                act.wait_ge(gu_full, i * FC + (c + 1))
                nc.scalar.activation(gate_tanh[:, c % 2, :], gate_bank(c), ACT.Tanh,
                                     scale=tanh_scale[:, c:c + 1]).then_inc(gtanh_made, 1)
                act.wait_ge(hidden_made, i * FC + (c + 1))
                nc.scalar.activation(hid_hi[:, c, :], hidden[:, c % 2, :], ACT.Copy).then_inc(hi_made, 1)

            def finish_group(i):
                for n, (t, lo, hi) in enumerate(PIECES):
                    act.wait_ge(halfy_made, i * PC + (n + 1))
                    nc.scalar.activation(y_tanh[:, n % 2, lo:hi], half_y[:, n % 2, lo:hi],
                                         ACT.Tanh).then_inc(ytanh_made, 1)

            act.sem_inc(attn_read, PRIMED)
            act.sem_inc(attn_done, PRIMED)
            act.dma_start(gate_s_sb[:], gate_s).then_inc(scales_loaded, 16)
            act.dma_start(up_s_sb[:], up_s).then_inc(scales_loaded, 16)
            act.dma_start(bqkv_sb[:], bqkv).then_inc(bqkv_loaded, 16)

            junk = probs[:].rearrange("p t s -> p (t s)")
            half = 3 * D * HC // 2
            for n in range(2):
                act.wait_ge(wqkv_loaded[n], 16)
                nc.scalar.activation(junk[:, bass.ts(n, half)], wqkv_sb[:].rearrange("p c f -> p (c f)")[:, bass.ts(n, half)],
                                     ACT.Square, accum_out=square_parts[:, 3 * n:3 * n + 1]).then_inc(squares_made, 1)
            act.wait_ge(wo_loaded, 16)
            nc.scalar.activation(junk[:, 3 * H:4 * H], wo_sb[:], ACT.Square,
                                 accum_out=square_parts[:, 1:2]).then_inc(squares_made, 1)
            act.wait_ge(bqkv_loaded, 16)
            nc.scalar.activation(qkv_hi[:, 0, 0:3], bqkv_sb[:], ACT.Square, scale=QKV_SCALE,
                                 accum_out=square_parts[:, 4:5]).then_inc(squares_made, 1)
            act.wait_ge(gu_scale_made, 1)
            nc.scalar.activation(qkv_hi[:, 1, 0:FC], gu_scale[:], ACT.Square,
                                 accum_out=square_parts[:, 2:3]).then_inc(squares_made, 1)
            evacuate_xt(0, range(0, 2), first=True)
            act.wait_ge(norm_step, NORM_STEPS)
            for n in range(3):
                if n == 1:
                    evacuate_xt(0, range(2, HC))
                nc.scalar.activation(wqkv_hi[:, :, bass.ts(n, D)], wqkv_sb[:, :, bass.ts(n, D)], ACT.Copy,
                                     scale=w_scale[:, 0:1]).then_inc(wqkv_hi_made, 1)
            nc.scalar.activation(wo_hi[:], wo_sb[:], ACT.Copy, scale=w_scale[:, 1:2]).then_inc(wo_hi_made, 1)
            act.wait_ge(bias_made, 1)
            act.wait_ge(wqkv_lo_made, 3)
            evacuate_q(0, first=True)
            evacuate_k(0)
            turn_weights(0, 0)
            evacuate_v(0)
            turn_weights(0, 1)
            with act.Fori(0, B - 1) as b:
                evacuate_xt(b + 1)
                exponentials(b)
                turn_weights(b, 2)
                evacuate_q(b + 1)
                evacuate_k(b + 1)
                take_pt_hi(b, range(TT))
                turn_weights(b + 1, 0)
                evacuate_o(b, KO_BANK)
                evacuate_v(b + 1)
                turn_weights(b + 1, 1)
                evacuate_attn(b, row_bank)
            turn_weights(B - 1, 2)
            exponentials(B - 1)
            act.wait_ge(w_cast, 3 * B)
            act.wait_ge(scales_made, 2)
            gate_chunk(0, 0)
            gate_chunk(0, 1)
            take_pt_hi(B - 1, range(0, 2))
            gate_chunk(0, 2)
            take_pt_hi(B - 1, range(2, TT))
            gate_chunk(0, 3)
            evacuate_o(B - 1, LAST_O_BANK)
            gate_chunk(0, 4)
            evacuate_attn(B - 1, last_wo_bank)
            for c in range(5, FC):
                gate_chunk(0, c)
            finish_group(0)
            with act.Fori(1, B) as i:
                for c in range(FC):
                    gate_chunk(i, c)
                finish_group(i)

        @block.vector
        def _(dve):
            LN_STEPS = 14

            def layernorm_stats(b, tiles=range(TT)):
                for t in tiles:
                    dve.wait_ge(x_loaded[t], (b + 1) * 16)
                    last = nc.vector.bn_stats(stats[:, t, :], x_sb[:, t, :])
                if t == TT - 1:
                    last.then_inc(ln_step, 1)

            def layernorm_variance(b):
                mean_e, mean_o = stats[:, :, 1], stats[:, :, 4]
                dve.wait_ge(ln_step, b * LN_STEPS + 1)
                nc.vector.tensor_tensor(mean_gap[:], mean_e, mean_o, ALU.subtract)
                nc.vector.tensor_tensor(mean_sum[:], mean_e, mean_o, ALU.add)
                nc.vector.tensor_tensor(square_sum[:], stats[:, :, 2], stats[:, :, 5], ALU.add).then_inc(ln_step, 1)
                dve.wait_ge(ln_step, b * LN_STEPS + 2)
                nc.vector.scalar_tensor_tensor(out=gap_square[:], in0=mean_gap[:], scalar=0.25, in1=mean_gap[:],
                                               op0=ALU.mult, op1=ALU.mult)
                nc.vector.tensor_scalar(mean[:], mean_sum[:], 0.5, None, ALU.mult)
                nc.vector.tensor_scalar(var[:], square_sum[:], 1.0 / H, EPS, ALU.mult, ALU.add).then_inc(ln_step, 1)
                dve.wait_ge(ln_step, b * LN_STEPS + 3)
                nc.vector.tensor_tensor(var_eps[:], var[:], gap_square[:], ALU.add).then_inc(ln_step, 1)
                dve.wait_ge(ln_step, b * LN_STEPS + 4)
                nc.vector.tensor_scalar(rs_y[:, 0, :].bitcast(I32), var_eps[:].bitcast(I32), -0.5, float(RSQRT_MAGIC),
                                        ALU.mult, ALU.add).then_inc(ln_step, 1)

            def layernorm_newton(b):
                for k in range(3):
                    dve.wait_ge(ln_step, b * LN_STEPS + (5 + 3 * k))
                    if k == 2:
                        nc.vector.tensor_scalar(rs_scaled[:], rs_y[:, 2, :], XN_SCALE, None, ALU.mult)
                    nc.vector.tensor_tensor(rs_t[:, k, :], rs_y[:, k, :], rs_y[:, k, :],
                                            ALU.mult).then_inc(ln_step, 1)
                    dve.wait_ge(ln_step, b * LN_STEPS + (6 + 3 * k))
                    nc.vector.scalar_tensor_tensor(out=rs_u[:, k, :], in0=rs_t[:, k, :], scalar=-0.5,
                                                   in1=var_eps[:], op0=ALU.mult, op1=ALU.mult).then_inc(ln_step, 1)
                    dve.wait_ge(ln_step, b * LN_STEPS + (7 + 3 * k))
                    new, old = (rstd[:], rs_scaled[:]) if k == 2 else (rs_y[:, k + 1, :], rs_y[:, k, :])
                    nc.vector.scalar_tensor_tensor(out=new, in0=rs_u[:, k, :], scalar=1.5, in1=old,
                                                   op0=ALU.add, op1=ALU.mult).then_inc(ln_step, 1)

            def layernorm_apply(b, first=False):
                dve.wait_ge(ln_step, (b + 1) * LN_STEPS)
                if not first:
                    dve.wait_ge(xt_full, b * HC)
                for t in range(TT):
                    nc.vector.tensor_scalar(xn[:, t, :], x_sb[:, t, :], mean[:, t:t + 1], rstd[:, t:t + 1],
                                            ALU.subtract, ALU.mult).then_inc(xn_made, 1)

            def take_xn_hi(b, chunks=range(HC)):
                for j in chunks:
                    dve.wait_ge(xt_read, b * HC + (j + 1))
                    nc.vector.tensor_copy(xn_hi[:, b, j, :], xnT[:, j, :]).then_inc(xhi_made, 1)

            def take_qkv_hi(b, n):
                dve.wait_ge((q_read, k_read, v_read)[n], b + 1)
                nc.vector.tensor_copy(qkv_hi[:, n, :], qkv_f32[:, n, :]).then_inc(qkv_hi_made, 1)

            def row_maximum(b, t):
                dve.wait_ge(scores_full, b * TT + (t + 1))
                nc.vector.reduce_max(row_max[:, t:t + 1], row_bank(t), AX_X).then_inc(max_made, 1)

            def negate_maximum(b, t):
                dve.wait_ge(max_made, b * TT + (t + 1))
                nc.vector.tensor_scalar(neg_max[:, t:t + 1], row_max[:, t:t + 1], neg_score_scale[:], None,
                                        ALU.mult).then_inc(negmax_made, 1)

            def invert_sum(b, t):
                dve.wait_ge(exp_made, b * TT + (t + 1))
                nc.vector.reciprocal(inv_sum[:, t:t + 1], row_sum[:, t:t + 1]).then_inc(inv_made, 1)

            def normalize(b, t):
                dve.wait_ge(inv_made, b * TT + (t + 1))
                nc.vector.tensor_scalar(probs[:, t, :], probs[:, t, :], inv_sum[:, t:t + 1], PROBS_SCALE,
                                        ALU.mult, ALU.mult).then_inc(probs_made, 1)

            def softmax(b):
                row_maximum(b, 0)
                negate_maximum(b, 0)
                row_maximum(b, 1)
                row_maximum(b, 2)
                negate_maximum(b, 1)
                invert_sum(b, 0)
                negate_maximum(b, 2)
                row_maximum(b, 3)
                normalize(b, 0)
                negate_maximum(b, 3)
                invert_sum(b, 1)
                invert_sum(b, 2)
                normalize(b, 1)
                normalize(b, 2)
                invert_sum(b, 3)
                normalize(b, 3)

            def take_pt_lo(b, chunks):
                for j in chunks:
                    dve.wait_ge(pt_hi_made, b * TT + (j + 1))
                    nc.vector.tensor_tensor(pt_lo[:, j, :], turn_bank(j), pt_hi[:, j, :],
                                            ALU.subtract).then_inc(pt_lo_made, 1)

            def split_o(b):
                dve.wait_ge(o_read, b + 1)
                nc.vector.tensor_copy(oT_hi[:], o_f32[:]).then_inc(o_hi_made, 1)
                dve.wait_ge(o_hi_made, b + 1)
                nc.vector.tensor_tensor(oT_lo[:], o_f32[:], oT_hi[:], ALU.subtract).then_inc(o_lo_made, 1)

            def finish_attn(b, bank):
                for t in range(HT, TT):
                    dve.wait_ge(wo_full, b * TT + (t + 1))
                    nc.vector.scalar_tensor_tensor(out=attn[:, b, t, :], in0=bank(t), scalar=attn_scale[:],
                                                   in1=bo_row[:], op0=ALU.mult, op1=ALU.add).then_inc(attn_done, 1)

            def attend(b, with_layernorm):
                take_xn_hi(b + 1)
                softmax(b)
                take_qkv_hi(b + 1, 0)
                if with_layernorm:
                    layernorm_stats(b + 2, range(0, 2))
                take_pt_lo(b, range(0, 2))
                take_qkv_hi(b + 1, 1)
                if with_layernorm:
                    layernorm_stats(b + 2, range(2, TT))
                    layernorm_variance(b + 2)
                take_pt_lo(b, range(2, TT))
                if with_layernorm:
                    layernorm_newton(b + 2)
                split_o(b)
                take_qkv_hi(b + 1, 2)
                if with_layernorm:
                    layernorm_apply(b + 2)
                finish_attn(b, row_bank)

            def gate_chunk(i, c):
                dve.wait_ge(gtanh_made, i * FC + (c + 1))
                nc.vector.scalar_tensor_tensor(out=gate_act[:, c % 2, :], in0=gate_tanh[:, c % 2, :], scalar=1.0,
                                               in1=gate_bank(c), op0=ALU.add, op1=ALU.mult).then_inc(gact_made, 1)
                dve.wait_ge(gact_made, i * FC + (c + 1))
                if c >= 2:
                    dve.wait_ge(lo_made, i * FC + (c - 1))
                nc.vector.scalar_tensor_tensor(out=hidden[:, c % 2, :], in0=gate_act[:, c % 2, :],
                                               scalar=hid_scale[:, c:c + 1], in1=up_bank(c),
                                               op0=ALU.mult, op1=ALU.mult).then_inc(hidden_made, 1)

            def finish_group(i):
                for n, (t, lo, hi) in enumerate(PIECES):
                    dve.wait_ge(down_full, i * PC + (n + 1))
                    if n >= 2:
                        dve.wait_ge(mixed_made, i * PC + (n - 1))
                    nc.vector.tensor_tensor(half_y[:, n % 2, lo:hi], down_bank(n, lo, hi), half_down_s[:, lo:hi],
                                            ALU.mult).then_inc(halfy_made, 1)
                    dve.wait_ge(halfy_made, i * PC + (n + 1))
                    if t < HT:
                        dve.wait_ge(attn_made, i * HT + (t + 1))
                    else:
                        dve.wait_ge(attn_done, i * HT + (t - HT + 1) + PRIMED)
                    nc.vector.tensor_tensor(half_mix[:, n % 2, lo:hi], half_y[:, n % 2, lo:hi],
                                            attn[:, i, t, lo:hi], ALU.mult).then_inc(halfmix_made, 1)
                    dve.wait_ge(ytanh_made, i * PC + (n + 1))
                    dve.wait_ge(halfmix_made, i * PC + (n + 1))
                    nc.vector.scalar_tensor_tensor(out=mixed[:, n % 2, lo:hi], in0=y_tanh[:, n % 2, lo:hi],
                                                   scalar=1.0, in1=half_mix[:, n % 2, lo:hi], op0=ALU.add,
                                                   op1=ALU.mult).then_inc(mixed_made, 1)
                    dve.wait_ge(mixed_made, i * PC + (n + 1))
                    dve.wait_ge(x_loaded[t], (i + (B + 1)) * 16)
                    nc.vector.tensor_tensor(out_sb[:, t, lo:hi], mixed[:, n % 2, lo:hi], x_sb[:, t, lo:hi],
                                            ALU.add).then_inc(out_made, 1)

            layernorm_stats(0)
            dve.wait_ge(scales_loaded, 32)
            nc.vector.tensor_tensor(gu_scale[:], gate_s_sb[:], up_s_sb[:], ALU.mult).then_inc(gu_scale_made, 1)
            layernorm_variance(0)
            layernorm_newton(0)
            layernorm_apply(0, first=True)

            dve.wait_ge(norms_full, 1)
            nc.vector.tensor_scalar(norm_guess[:], NORM_BANK.bitcast(I32), -0.5, float(RSQRT_MAGIC),
                                    ALU.mult, ALU.add).then_inc(norm_step, 1)
            dve.wait_ge(norm_step, 1)
            nc.vector.tensor_scalar(norm_inverse[:].bitcast(I32), norm_guess[:], EXPONENT_BITS, None,
                                    ALU.bitwise_and).then_inc(norm_step, 1)
            dve.wait_ge(norm_step, 2)
            nc.vector.tensor_scalar(w_scale[:], norm_inverse[:], W_SCALE, None, ALU.mult).then_inc(norm_step, 1)
            dve.wait_ge(norm_step, NORM_STEPS)
            take_xn_hi(0, range(0, 2))
            for n in range(3):
                if n == 1:
                    take_xn_hi(0, range(2, HC))
                dve.wait_ge(wqkv_hi_made, n + 1)
                nc.vector.scalar_tensor_tensor(out=wqkv_lo[:, :, bass.ts(n, D)], in0=wqkv_sb[:, :, bass.ts(n, D)],
                                               scalar=w_scale[:, 0:1], in1=wqkv_hi[:, :, bass.ts(n, D)],
                                               op0=ALU.mult, op1=ALU.subtract).then_inc(wqkv_lo_made, 1)
            nc.vector.tensor_scalar(w_unscale[:].bitcast(I32), w_scale[:].bitcast(I32), -1.0, float(0x7F000000),
                                    ALU.mult, ALU.add).then_inc(norm_step, 1)
            nc.vector.tensor_scalar(bias[:], bqkv_sb[:], w_scale[:, 0:1], QKV_SCALE, ALU.mult,
                                    ALU.mult).then_inc(bias_made, 1)
            layernorm_stats(1)
            layernorm_variance(1)
            take_qkv_hi(0, 0)
            layernorm_newton(1)
            take_qkv_hi(0, 1)
            layernorm_apply(1)
            dve.wait_ge(wo_hi_made, 1)
            nc.vector.scalar_tensor_tensor(out=wo_lo[:], in0=wo_sb[:], scalar=w_scale[:, 1:2], in1=wo_hi[:],
                                           op0=ALU.mult, op1=ALU.subtract).then_inc(wo_lo_made, 1)
            dve.wait_ge(norm_step, NORM_STEPS + 1)
            nc.vector.tensor_scalar(score_scale[:], w_unscale[:, 0:1], w_unscale[:, 0:1],
                                    SM_SCALE / QKV_SCALE / QKV_SCALE, ALU.mult, ALU.mult)
            nc.vector.tensor_scalar(neg_score_scale[:], w_unscale[:, 0:1], w_unscale[:, 0:1],
                                    -SM_SCALE / QKV_SCALE / QKV_SCALE, ALU.mult, ALU.mult)
            nc.vector.tensor_scalar(attn_scale[:], w_unscale[:, 0:1], w_unscale[:, 1:2], 1.0 / QKV_SCALE,
                                    ALU.mult, ALU.mult).then_inc(norm_step, 1)

            nc.vector.tensor_scalar(tanh_scale[:], gate_s_sb[:], 0.5 / XN_SCALE, None,
                                    ALU.mult).then_inc(scales_made, 1)
            nc.vector.tensor_scalar(hid_scale[:], gu_scale[:], w_scale[:, 2:3],
                                    0.5 * HID_SCALE / XN_SCALE / XN_SCALE, ALU.mult,
                                    ALU.mult).then_inc(scales_made, 1)
            take_qkv_hi(0, 2)
            dve.wait_ge(rows_loaded, 32)
            nc.vector.tensor_scalar(half_down_s[:], half_down_s[:], w_unscale[:, 2:3], 0.5 / HID_SCALE, ALU.mult,
                                    ALU.mult).then_inc(rows_made, 1)
            dve.wait_ge(norm_step, NORM_STEPS + 2)
            dve.wait_ge(scales_made, 2)
            dve.wait_ge(rows_made, 1)

            with dve.Fori(0, B - 2) as b:
                attend(b, True)
            attend(B - 2, False)

            softmax(B - 1)
            gate_chunk(0, 0)
            gate_chunk(0, 1)
            take_pt_lo(B - 1, range(0, 2))
            gate_chunk(0, 2)
            take_pt_lo(B - 1, range(2, TT))
            gate_chunk(0, 3)
            split_o(B - 1)
            gate_chunk(0, 4)
            gate_chunk(0, 5)
            finish_attn(B - 1, last_wo_bank)
            for c in range(6, FC):
                gate_chunk(0, c)
            finish_group(0)
            with dve.Fori(1, B) as i:
                for c in range(FC):
                    gate_chunk(i, c)
                finish_group(i)

        @block.tensor
        def _(pe):
            def products(out, terms):
                for n, (stationary, moving) in enumerate(terms):
                    last = nc.tensor.matmul(out, stationary, moving, start=(n == 0), stop=(n == len(terms) - 1))
                return last

            def transpose_xn(b):
                for j in range(HC):
                    if j >= 2:
                        pe.wait_ge(xt_read, b * HC + (j - 1))
                    for t in range(TT):
                        if j == 0:
                            pe.wait_ge(xn_made, b * TT + (t + 1))
                        last = nc.tensor.transpose(turn_bank(j)[:, bass.ts(t, P)], xn[:, t, bass.ts(j, P)],
                                                   identity[:])
                    last.then_inc(xt_full, 1)

            def project_q_or_k(b, n, bank, full):
                cols = bass.ts(n, D)
                for j in range(HC):
                    if n == 0:
                        pe.wait_ge(xhi_made, b * HC + (j + 1))
                    nc.tensor.matmul(bank, wqkv_hi[:, j, cols], xn_hi[:, b, j, :], start=(j == 0), stop=False)
                    nc.tensor.matmul(bank, wqkv_lo[:, j, cols], xn_hi[:, b, j, :], start=False, stop=False)
                for j in range(HC):
                    if n == 0:
                        pe.wait_ge(xlo_made, b * HC + (j + 1))
                    last = nc.tensor.matmul(bank, wqkv_hi[:, j, cols], xn_lo[:, b, j, :], start=False,
                                            stop=(j == HC - 1))
                last.then_inc(full, 1)

            def project_q(b, first=False):
                if not first:
                    pe.wait_ge(v_read, b)
                project_q_or_k(b, 0, QV_BANK, q_full)

            def project_k(b):
                project_q_or_k(b, 1, KO_BANK, k_full)

            def project_v(b, tiles):
                cols = bass.ts(2, D)
                for t in tiles:
                    if t == 0:
                        pe.wait_ge(q_read, b + 1)
                    rows = bass.ts(t, P)
                    last = products(QV_BANK[:, bass.ts(t, D)],
                                    [(half[:, b, j, rows], w[:, j, cols]) for j in range(HC)
                                     for half, w in ((xn_hi, wqkv_hi), (xn_hi, wqkv_lo), (xn_lo, wqkv_hi))])
                    if t == TT - 1:
                        last.then_inc(v_full, 1)

            def scores(b):
                pe.wait_ge(qkv_lo_made, b * 3 + 2)
                for t in range(TT):
                    pe.wait_ge(attn_read if t < HT else attn_done, b * HT + (t % HT + 1 - HT) + PRIMED)
                    cols = bass.ts(t, P)
                    products(row_bank(t), [(qkv_hi[:, 0, cols], qkv_hi[:, 1, :]), (qkv_hi[:, 0, cols], qkv_lo[:, 1, :]),
                                           (qkv_lo[:, 0, cols], qkv_hi[:, 1, :])]).then_inc(scores_full, 1)

            def transpose_probs(b, chunks):
                for j in chunks:
                    if j >= 2:
                        pe.wait_ge(pt_lo_made, b * TT + (j - 1))
                    for t in range(TT):
                        if j == 0:
                            pe.wait_ge(probs_made, b * TT + (t + 1))
                        last = nc.tensor.transpose(turn_bank(j)[:, bass.ts(t, P)], probs[:, t, bass.ts(j, P)],
                                                   identity[:])
                    last.then_inc(pt_full, 1)

            def probs_times_v(b, bank):
                pe.wait_ge(qkv_lo_made, (b + 1) * 3)
                for j in range(TT):
                    cols = bass.ts(j, D)
                    pe.wait_ge(pt_hi_made, b * TT + (j + 1))
                    nc.tensor.matmul(bank, qkv_hi[:, 2, cols], pt_hi[:, j, :], start=(j == 0), stop=False)
                    nc.tensor.matmul(bank, qkv_lo[:, 2, cols], pt_hi[:, j, :], start=False, stop=False)
                for j in range(TT):
                    cols = bass.ts(j, D)
                    pe.wait_ge(pt_lo_made, b * TT + (j + 1))
                    last = nc.tensor.matmul(bank, qkv_hi[:, 2, cols], pt_lo[:, j, :], start=False, stop=(j == TT - 1))
                last.then_inc(o_full, 1)

            def project_o(b, tiles, bank, bank_free):
                pe.wait_ge(wo_lo_made, 1)
                for t in tiles:
                    rows = bass.ts(t, P)
                    bank_free(t)
                    pe.wait_ge(o_hi_made, b + 1)
                    nc.tensor.matmul(bank(t), oT_hi[:, rows], wo_hi[:], start=True, stop=False)
                    nc.tensor.matmul(bank(t), oT_hi[:, rows], wo_lo[:], start=False, stop=False)
                    pe.wait_ge(o_lo_made, b + 1)
                    nc.tensor.matmul(bank(t), oT_lo[:, rows], wo_hi[:], start=False, stop=True).then_inc(wo_full, 1)

            def gate_chunk(i, c):
                if c >= 2:
                    pe.wait_ge(hidden_made, i * FC + (c - 1))
                for bank, w in ((gate_bank(c), gate_w), (up_bank(c), up_w)):
                    last = products(bank, [(w[:, j, bass.ts(c, P)], half[:, i, j, :])
                                           for j in range(HC) for half in (xn_hi, xn_lo)])
                last.then_inc(gu_full, 1)

            def down_group(i):
                for n, (t, lo, hi) in enumerate(PIECES):
                    if n >= 2:
                        pe.wait_ge(halfy_made, i * PC + (n - 1))
                    for c in range(FC):
                        if n == 0:
                            pe.wait_ge(lo_made, i * FC + (c + 1))
                        for half in (hid_hi, hid_lo):
                            last = nc.tensor.matmul(down_bank(n, lo, hi), half[:, c, bass.ts(t, P)],
                                                    down_w[:, c, lo:hi], start=(c == 0 and half is hid_hi),
                                                    stop=(c == FC - 1 and half is hid_lo))
                    last.then_inc(down_full, 1)

            pe.wait_ge(ones_made, 1)
            for _ in range(WARM_UP):
                nc.tensor.matmul(WARM_BANK, ones[:], ones[:], start=True, stop=True)
            pe.wait_ge(squares_made, 5)
            nc.tensor.matmul(NORM_BANK, ones[:], square_parts[:, 0:3], start=True, stop=False)
            nc.tensor.matmul(NORM_BANK[:, 0:1], ones[:], square_parts[:, 3:4], start=False, stop=False)
            nc.tensor.matmul(NORM_BANK[:, 0:1], ones[:], square_parts[:, 4:5], start=False,
                             stop=True).then_inc(norms_full, 1)
            pe.wait_ge(identity_made, 2)
            transpose_xn(0)
            pe.wait_ge(wqkv_lo_made, 1)
            project_q(0, first=True)
            pe.wait_ge(wqkv_lo_made, 2)
            project_k(0)
            pe.wait_ge(wqkv_lo_made, 3)
            project_v(0, range(TT))
            with pe.Fori(0, B - 1) as b:
                transpose_xn(b + 1)
                scores(b)
                project_q(b + 1)
                project_k(b + 1)
                transpose_probs(b, range(0, 2))
                project_v(b + 1, range(0, TT // 2))
                transpose_probs(b, range(2, TT))
                pe.wait_ge(k_read, b + 2)
                probs_times_v(b, KO_BANK)
                project_v(b + 1, range(TT // 2, TT))
                project_o(b, range(TT), row_bank, lambda t: None)

            scores(B - 1)
            pe.wait_ge(w_cast, 3 * B)
            pe.wait_ge(v_read, B)
            pe.wait_ge(o_read, B - 1)
            gate_chunk(0, 0)
            pe.wait_ge(exp_made, TT * B)
            gate_chunk(0, 1)
            transpose_probs(B - 1, range(0, 2))
            gate_chunk(0, 2)
            transpose_probs(B - 1, range(2, TT))
            gate_chunk(0, 3)
            probs_times_v(B - 1, LAST_O_BANK)
            gate_chunk(0, 4)

            def last_wo_free(t):
                if t >= 2:
                    pe.wait_ge(attn_read, HT * (B - 1) + (t - 1) + PRIMED)

            project_o(B - 1, range(0, 2), last_wo_bank, last_wo_free)
            gate_chunk(0, 5)
            project_o(B - 1, range(2, TT), last_wo_bank, last_wo_free)
            for c in range(6, FC):
                gate_chunk(0, c)
            pe.wait_ge(attn_done, HT * B + PRIMED)
            down_group(0)
            with pe.Fori(1, B) as i:
                for c in range(FC):
                    gate_chunk(i, c)
                down_group(i)


def kernel(**inputs):
    import numpy as np
    import concourse.bacc as bacc
    from concourse.bass_utils import run_bass_kernel_spmd

    a = {name.removeprefix("L0_"): np.asarray(value) for name, value in inputs.items()}
    B, S, H = a["attn_x"].shape
    FF = a["ffn_gate_t"].shape[0]
    arrays = {
        "x": a["attn_x"],
        "wqkv": a["attn_Wqkv"],
        "bqkv": a["attn_bqkv"].reshape(3, P).T,
        "wo": a["attn_Wo"],
        "bo": a["attn_bo"].reshape(1, H),
        "gate_t": a["ffn_gate_t"].T,
        "up_t": a["ffn_up_t"].T,
        "down_t": a["ffn_down_t"].reshape(B, H // B, FF // P, P).transpose(0, 3, 2, 1).reshape(B, P, FF),
        "gate_s": a["ffn_gate_s"].reshape(FF // P, P).T,
        "up_s": a["ffn_up_s"].reshape(FF // P, P).T,
        "down_s": a["ffn_down_s"].reshape(1, H),
    }
    nc = bacc.Bacc("TRN2", target_bir_lowering=False, num_devices=1)
    named, args = {}, []
    for name, value in arrays.items():
        value = np.ascontiguousarray(value)
        named[f"in_{name}"] = value
        args.append(nc.dram_tensor(f"in_{name}", value.shape, mybir.dt.from_np(value.dtype), kind="ExternalInput").ap())
    args.append(nc.dram_tensor("out_0", (B, S, H), F32, kind="ExternalOutput").ap())
    gated_attention_ffn(nc, *args)
    result = run_bass_kernel_spmd(nc, [named], core_ids=[0])
    return result.results[0]["out_0"]
```
